# Optimizing a Trainium2 kernel written in Bass

```python
import numpy as np
import jax
import jax.numpy as jnp

def _softmax(x, axis=-1):
    return jax.nn.softmax(x, axis=axis)

def _gelu(x):
    return jax.nn.gelu(x, approximate=True)

def _silu(x):
    return jax.nn.silu(x)

def _sigmoid(x):
    return jax.nn.sigmoid(x)

def _layernorm(x, axis=-1, eps=1e-05):
    m = jnp.mean(x, axis=axis, keepdims=True)
    v = jnp.var(x, axis=axis, keepdims=True)
    return (x - m) / jnp.sqrt(v + eps)

def _scatter_add(tgt, idx, src, axis=0):
    return tgt.at[idx].add(src)

def _segment_sum(src, seg, n):
    return jax.ops.segment_sum(src, seg, n)
kernel_name = 'mk_seq_postln_d1_jaxref_r8_49c361'

def setup_inputs(seed: int=0):
    np.random.seed(seed)
    _w = jnp.asarray

    def _L0_attn_setup():
        import jax, jax.numpy as jnp
        import numpy as np
        N_HEAD = 16
        N_EMBED = 256
        N_BLOCK = 256
        THETA = 10000.0

        def _rope_cos_sin(n_head, head_dim):
            freqs = THETA ** (-(jnp.arange(0, head_dim, 2, dtype=jnp.float32) / head_dim))
            t = jnp.arange(n_head, dtype=jnp.float32)
            ang = jnp.outer(t, freqs)
            return (jnp.cos(ang)[None, :, None, :], jnp.sin(ang)[None, :, None, :])

        def _apply_rope(x, cos, sin):
            B, H, T, hd = x.shape
            xp = x.reshape(B, H, T, hd // 2, 2)
            a, b = (xp[..., 0], xp[..., 1])
            out = jnp.stack([a * cos - b * sin, a * sin + b * cos], axis=-1)
            return out.reshape(B, H, T, hd)
        key = jax.random.key(seed)
        ks = jax.random.split(key, 5)
        E = N_EMBED
        x = jax.random.normal(ks[0], (2, 256, E), dtype=jnp.float32)
        s = 1.0 / np.sqrt(E)
        w_attn = jax.random.normal(ks[1], (E, 3 * E), dtype=jnp.float32) * s
        b_attn = jnp.zeros((3 * E,), dtype=jnp.float32)
        w_proj = jax.random.normal(ks[2], (E, E), dtype=jnp.float32) * s
        b_proj = jnp.zeros((E,), dtype=jnp.float32)
        return {'x': x, 'w_attn': w_attn, 'b_attn': b_attn, 'w_proj': w_proj, 'b_proj': b_proj}
    _L0_attn_in = _L0_attn_setup()

    def _L0_ffn_setup():
        import jax, jax.numpy as jnp
        import numpy as np
        D_MODEL = 256
        FFN = 512
        N_EXPERTS = 8
        TOP_K = 2
        key = jax.random.key(seed)
        k1, k2, k3, k4 = jax.random.split(key, 4)
        scale = 0.02
        hidden_states = jax.random.normal(k1, (4, 128, D_MODEL), dtype=jnp.float32)
        router_w = jax.random.normal(k2, (N_EXPERTS, D_MODEL), dtype=jnp.float32) * scale
        ws = jax.random.normal(k3, (N_EXPERTS, 2 * FFN, D_MODEL), dtype=jnp.float32) * scale
        w2s = jax.random.normal(k4, (N_EXPERTS, D_MODEL, FFN), dtype=jnp.float32) * scale
        return {'hidden_states': hidden_states, 'router_w': router_w, 'ws': ws, 'w2s': w2s}
    _L0_ffn_in = _L0_ffn_setup()
    _d = {'L0_attn_x': _L0_attn_in['x'], 'L0_attn_w_attn': _L0_attn_in['w_attn'], 'L0_attn_b_attn': _L0_attn_in['b_attn'], 'L0_attn_w_proj': _L0_attn_in['w_proj'], 'L0_attn_b_proj': _L0_attn_in['b_proj'], 'L0_ffn_router_w': _L0_ffn_in['router_w'], 'L0_ffn_ws': _L0_ffn_in['ws'], 'L0_ffn_w2s': _L0_ffn_in['w2s']}
    _x0 = _d['L0_attn_x']
    _d['L0_attn_x'] = jax.random.normal(jax.random.fold_in(jax.random.key(seed), 1), (4, 512, 256), dtype=_x0.dtype)
    del _x0
    return _d

def reference(L0_attn_x, L0_attn_w_attn, L0_attn_b_attn, L0_attn_w_proj, L0_attn_b_proj, L0_ffn_router_w, L0_ffn_ws, L0_ffn_w2s):

    def _L0_attn_ref(x, w_attn, b_attn, w_proj, b_proj):
        import jax, jax.numpy as jnp
        import numpy as np
        N_HEAD = 16
        N_EMBED = 256
        N_BLOCK = 256
        THETA = 10000.0

        def _rope_cos_sin(n_head, head_dim):
            freqs = THETA ** (-(jnp.arange(0, head_dim, 2, dtype=jnp.float32) / head_dim))
            t = jnp.arange(n_head, dtype=jnp.float32)
            ang = jnp.outer(t, freqs)
            return (jnp.cos(ang)[None, :, None, :], jnp.sin(ang)[None, :, None, :])

        def _apply_rope(x, cos, sin):
            B, H, T, hd = x.shape
            xp = x.reshape(B, H, T, hd // 2, 2)
            a, b = (xp[..., 0], xp[..., 1])
            out = jnp.stack([a * cos - b * sin, a * sin + b * cos], axis=-1)
            return out.reshape(B, H, T, hd)
        B, T, E = x.shape
        H = N_HEAD
        hd = E // H
        qkv = x @ w_attn + b_attn
        q, k, v = jnp.split(qkv, 3, axis=-1)
        q = q.reshape(B, T, H, hd).transpose(0, 2, 1, 3)
        k = k.reshape(B, T, H, hd).transpose(0, 2, 1, 3)
        v = v.reshape(B, T, H, hd).transpose(0, 2, 1, 3)
        cos, sin = _rope_cos_sin(H, hd)
        q = _apply_rope(q, cos, sin)
        k = _apply_rope(k, cos, sin)
        scores = jnp.einsum('bhtd,bhsd->bhts', q, k)
        causal = jnp.tril(jnp.ones((T, T), dtype=bool))
        scores = jnp.where(causal[None, None], scores, jnp.float32(-jnp.inf))
        attn = jax.nn.softmax(scores, axis=-1) * E ** (-0.5)
        o = jnp.einsum('bhts,bhsd->bhtd', attn, v)
        o = o.transpose(0, 2, 1, 3).reshape(B, T, E)
        return o @ w_proj + b_proj

    def _L0_ffn_ref(hidden_states, router_w, ws, w2s):
        import jax, jax.numpy as jnp
        import numpy as np
        D_MODEL = 256
        FFN = 512
        N_EXPERTS = 8
        TOP_K = 2
        B, S, D = hidden_states.shape
        x = hidden_states.reshape(-1, D)
        T = x.shape[0]
        E = router_w.shape[0]
        I = ws.shape[1] // 2
        logits = x @ router_w.T
        probs = jax.nn.softmax(logits.astype(jnp.float32), axis=-1)
        top_w, top_i = jax.lax.top_k(probs, TOP_K)
        top_w = top_w / jnp.sum(top_w, axis=-1, keepdims=True)
        combine = jnp.zeros((T, E), dtype=jnp.float32)
        combine = combine.at[jnp.arange(T)[:, None], top_i].add(top_w)
        combine = combine.astype(x.dtype)
        out = jnp.zeros((T, D), dtype=x.dtype)
        for e in range(E):
            gate = x @ ws[e, :I, :].T
            up = x @ ws[e, I:, :].T
            h = jax.nn.silu(gate) * up
            out = out + combine[:, e:e + 1] * (h @ w2s[e].T)
        return out.reshape(B, S, D)
    x = L0_attn_x
    x = _layernorm(x + _L0_attn_ref(x, L0_attn_w_attn, L0_attn_b_attn, L0_attn_w_proj, L0_attn_b_proj), axis=-1)
    x = _layernorm(x + _L0_ffn_ref(x, L0_ffn_router_w, L0_ffn_ws, L0_ffn_w2s), axis=-1)
    return x

_drawn_inputs = setup_inputs


def setup_inputs(seed=0):
    import zlib

    import numpy as np

    out = dict(_drawn_inputs(seed))
    spreads = {'L0_attn_b_attn': (0.0, 0.751), 'L0_attn_b_proj': (0.0, 0.1)}
    factors = {'L0_ffn_router_w': 3.812, 'L0_ffn_ws': 3.319, 'L0_ffn_w2s': 3.322}
    for name, (base, spread) in spreads.items():
        noise = np.random.default_rng([zlib.crc32(name.encode()), seed]).standard_normal(out[name].shape)
        drawn = base * np.exp(spread * noise) if base else spread * noise
        out[name] = jnp.asarray(drawn.astype(out[name].dtype))
    for name, factor in factors.items():
        out[name] = (out[name] * factor).astype(out[name].dtype)
    return out
```

```python
import concourse.bass as bass
from concourse import mybir
from contextlib import ExitStack
import numpy as np

F32 = mybir.dt.float32
BF16 = mybir.dt.bfloat16
I32 = mybir.dt.int32
U32 = mybir.dt.uint32
ALU = mybir.AluOpType
ACT = mybir.ActivationFunctionType
AX = mybir.AxisListType

P = 128
B, T, E = 4, 512, 256
H, HD = 16, 16
NTOK = B * T
NTT = NTOK // P
TT = T // P
KC = E // P
NG = 4
GH = H // NG
NU = B * NG
PARTS = 3
QPART = [0, 0, 0, 1, 1, 2]
KPART = [0, 1, 2, 0, 1, 0]
SK = HD * len(QPART)
SKM = SK + PARTS * GH
NX, FF, TOPK = 8, 512, 2
REGION = NTOK
NTILES = NTOK * TOPK // P + NX - 1
TRIO = 3
NTAB = NTILES + TRIO
NSLOT = NX * REGION + NTAB * P
EPS = 1e-5
NSG, NTG = 10, 5


class Tally:

    def __init__(self):
        self.base, self.n = 0, 0

    def step(self):
        self.n += 1
        return self.base + self.n

    def enter(self, trip, per):
        self.start, self.per, self.n = self.base + self.n, per, 0
        self.base = trip * per + self.start

    def leave(self, trips):
        assert self.n == self.per, (self.n, self.per)
        self.base, self.n = self.start + trips * self.per, 0


def block_kernel(nc, x, xT, w_attn, b_attn, w_proj, b_proj, router_wT, w1T, w2T, cos_sin, cf, cb, kones, tokid, out):
    ctx = ExitStack()
    with ctx:
        def sb(name, shape, dt=F32):
            return ctx.enter_context(nc.sbuf_tensor(name, shape, dt))

        def sem(name):
            return ctx.enter_context(nc.semaphore(name))

        def dram(name, shape, dt):
            return nc.dram_tensor(name, shape, dt, kind="Internal").ap()

        qk_dram = dram("qk_parts", (2, PARTS, E, NTOK), BF16)
        x1_dram = dram("x1_rows", (NTOK, E), F32)
        tok_dram = dram("slot_token", (NSLOT, 1), I32)
        y_dram = dram("tile_out", (NTILES * P, E), F32)

        W1 = sb("W1", [P, KC * NX * 2 * FF])
        W2 = sb("W2", [P, 4 * NX * E])
        w1 = W1[:, :].rearrange("p (k e f) -> p k e f", k=KC, e=NX)
        w2 = W2[:, :].rearrange("p (k e f) -> p k e f", k=4, e=NX)
        CF = sb("CF", [P, cf.shape[1]])
        ident, selE, selO = (CF[:, n * P:(n + 1) * P] for n in range(3))
        iota8, ebase8 = CF[:, 384:392], CF[:, 392:400]
        thr16, tri8, jidx = CF[:, 400:416], CF[:, 416:480], CF[:, 480:480 + NTAB]
        CB = sb("CB", [P, 5 * P], BF16)
        identb, maskS, maskT, tri, onesb = (CB[:, n * P:(n + 1) * P] for n in range(5))
        WP = sb("WP", [P, 2, E])
        RW = sb("RW", [P, KC, NX])
        BP = sb("BP", [P, E])
        VR = sb("VR", [P, NTT, E])
        X1 = sb("X1", [P, TT, E])
        WT = sb("WT", [P, NTT, TOPK])
        SLR = sb("SLR", [P, NTT * TOPK])
        ROW = sb("ROW", [P, NTT * TOPK], I32)
        GR = sb("GR", [P, NTT * TOPK, NX - 1])
        GR2 = sb("GR2", [P, NTT * TOPK, NX - 1])
        SH = sb("SH", [P, NX - 1])
        TOK = sb("TOK", [P, NTT], I32)
        TAB = sb("TAB", [1, 2, NTAB], I32)
        K = [sb(f"K{p}", [P, GH, T], BF16) for p in range(2)]
        Q = [sb(f"Q{p}", [P, GH, T], BF16) for p in range(2)]
        VA = [sb(f"VA{p}", [P, TT, GH, 32]) for p in range(2)]
        PT = [sb(f"PT{n}", [P, 2 * T]) for n in range(NTG)]
        O = [sb(f"O{p}", [P, T]) for p in range(2)]
        RC = sb("RC", [P, T])
        TMP = sb("TMP", [P, T])
        C = [sb(f"C{c}", [P, T]) for c in range(2)]
        MX = [sb(f"MX{p}", [P, GH, 8]) for p in range(2)]
        NM = sb("NM", [P, 2, TT, GH])
        NP = [sb(f"NP{p}", [P, TT, PARTS * GH], BF16) for p in range(2)]
        XB = sb("XB", [P, TT, E])
        ST6 = sb("ST6", [P, TT, 6])
        MV = sb("MV", [P, TT, 2])
        VE = sb("VE", [P, TT, 1])
        RS = sb("RS", [P, TT, 1])
        MHALF = sb("MHALF", [P, 1])
        XT1 = sb("XT1", [P, TT, KC, P])
        LG = sb("LG", [P, TT, NX])
        MVX = sb("MVX", [P, TT, 8])
        MIX = sb("MIX", [P, TT, 8], U32)
        MIF = sb("MIF", [P, TT, 8])
        OH = [sb(f"OH{k}", [P, TT, NX]) for k in range(TOPK)]
        MC = sb("MC", [P, TT, NX], BF16)
        MRUN = sb("MRUN", [P, NX], BF16)
        MSUM = sb("MSUM", [P, NX])
        DL = sb("DL", [P, TT])
        EX = sb("EX", [P, TT])
        SM = sb("SM", [P, TT])
        RK = sb("RK", [P, TT, NX])
        RKO = [sb(f"RKO{k}", [P, TT, NX]) for k in range(TOPK)]
        SLF = sb("SLF", [P, TT, TOPK])
        SLI = sb("SLI", [P, TT, TOPK], I32)
        TOK4 = sb("TOK4", [P, TT], I32)
        WB4 = sb("WB4", [P, TT, TOPK])
        WA = W1[:, 0:2304].rearrange("p (k f) -> p k f", k=3)
        WR = W1[:, 2304:3840].rearrange("p (k f) -> p k f", k=3)
        RT = W1[:, 3840:4096].rearrange("p (k f) -> p k f", k=2)
        RTMP = W1[:, 4096:5120].rearrange("p (k f) -> p k f", k=4)
        XTB = [W1[:, 5120 + 1024 * n:6144 + 1024 * n].rearrange("p (k t) -> p k t", k=KC) for n in range(B)]
        QF = [W1[:, 9216 + 512 * n:9728 + 512 * n] for n in range(4)]
        R1 = [W1[:, 11264 + 512 * n:11776 + 512 * n] for n in range(4)]
        PB = [W1[:, 13312 + 768 * n:14080 + 768 * n].bitcast(BF16).rearrange("p (r t) -> p r t", r=3) for n in range(4)]
        BC = sb("BC", [P, 4])
        ONE = sb("ONE", [P, 1])
        XG = [PT[0][:, 256 * n:256 * n + 256] for n in range(3)]
        XGT = PT[1][:, 0:256].rearrange("p (k t) -> p k t", k=KC)
        SIL, HH = PT[2][:, 0:512], PT[2][:, 512:1024]
        HT = PT[3][:, 0:512].rearrange("p (k t) -> p k t", k=4)
        YS = [PT[4][:, 256 * n:256 * n + 256] for n in range(3)]
        IDX = [sb(f"IDX{n}", [P, 1], I32) for n in range(3)]
        IDG = sb("IDG", [P, TT, TOPK], I32)
        ZI = sb("ZI", [P, NSLOT // P], I32)
        NF = sb("NF", [P, NX])
        GE = sb("GE", [P, NX, 16])
        NT = sb("NT", [P, NX])
        CT = sb("CT", [P, NX])
        G8 = sb("G8", [P, NX, NX])
        GJ = sb("GJ", [1, NTAB, NX])
        GP = sb("GP", [1, NTAB, NX])
        EJ = sb("EJ", [1, NTAB])
        PJ = sb("PJ", [1, NTAB])
        RJ = sb("RJ", [1, NTAB])

        PS = ctx.enter_context(nc.psum_tensor("PS", [P, 8, 512], F32))
        bank = [PS[:, n, :] for n in range(8)]
        Sb = [bank[0], bank[1]]
        STb = [PS[:, 2 + 2 * n:4 + 2 * n, :] for n in range(2)]
        Ob = bank[6]
        MISC = bank[7]
        miscb = MISC.bitcast(BF16)

        s_const, s_rope, s_x = sem("s_const"), sem("s_rope"), [sem(f"s_x{b}") for b in range(B)]
        s_sync = {n: sem("a_" + n) for n in ("init", "one", "dve", "wr", "bias", "bc", "ps", "vps", "qf", "h", "r", "m", "l", "v")}
        a = s_sync
        s_pb = [sem(f"s_pb{c}") for c in range(4)]

        names = ("S", "Sf", "red", "mx", "np", "pool", "qm", "ST", "exp", "pv", "ocp", "rc", "rb", "rbm", "pair", "va",
                 "mt", "ap", "res", "x1", "xb", "tp", "xt", "lgp", "lg", "mc", "rkp", "rk", "mrun", "dve", "dl", "ex", "slots",
                 "cnt", "var", "rs")
        s = {n: sem("b_" + n) for n in names}
        s_kq = [sem(f"s_kq{p}") for p in range(2)]
        s_xb, s_x1w, s_w, s_sc = sem("s_xb"), sem("s_x1w"), sem("s_w"), sem("s_sc")

        with nc.Block() as block:
            @block.sync
            def _(sp):
                sp.dma_start(WA[:, 0:2, :], w_attn.rearrange("(k p) f -> p k f", p=P)).then_inc(s_rope, 16)
                sp.dma_start(WA[:, 2, :], b_attn.partition_broadcast(P)).then_inc(s_rope, 16)
                sp.dma_start(RT, cos_sin.partition_broadcast(P)).then_inc(s_rope, 16)
                for b in range(B):
                    sp.dma_start(XTB[b], xT[:, b * T:(b + 1) * T].rearrange("(k p) t -> p k t", p=P)).then_inc(s_x[b], 16)
                for b in range(B):
                    for c in range(4):
                        sp.wait_ge(a["l"], 4 * b + c + 1)
                        sp.dma_start(qk_dram[c // 2, :, (c % 2) * P:(c % 2 + 1) * P, b * T:(b + 1) * T].rearrange("r p t -> p r t"),
                                     PB[c]).then_inc(s_pb[c], 16)
                for c in range(4):
                    sp.wait_ge(s_pb[c], 16 * B)

            @block.gpsimd
            def _(pool):
                pool.wait_ge(a["init"], 1)
                pool.dma_start(tok_dram.rearrange("(p n) o -> p (n o)", p=P), ZI[:, :]).then_inc(s_sc, 16)
                for b in range(B):
                    for c in range(4):
                        pool.wait_ge(a["r"], 4 * b + c + 1)
                        pool.tensor_copy(PB[c][:, 1, :], R1[c]).then_inc(a["m"], 1)
                pool.wait_ge(s_sc, 16)

            @block.scalar
            def _(act):
                act.dma_start(CF[:, :], cf).then_inc(s_const, 16)
                act.dma_start(CB[:, :], cb).then_inc(s_const, 16)
                for p in range(2):
                    act.dma_start(K[p][SK:SKM, :, :], kones).then_inc(s_const, 16)
                act.dma_start(WP[:, :, :], w_proj.rearrange("c p f -> p c f")).then_inc(s_const, 16)
                act.dma_start(RW[:, :, :], router_wT.rearrange("(k p) e -> p k e", p=P)).then_inc(s_const, 16)
                act.dma_start(BP[:, :], b_proj.partition_broadcast(P)).then_inc(s_const, 16)
                act.dma_start(TOK[:, :], tokid).then_inc(s_const, 16)
                act.wait_ge(a["bc"], 1)
                for b in range(B):
                    for c in range(4):
                        act.wait_ge(a["ps"], 4 * b + c + 1)
                        if b:
                            act.wait_ge(a["l"], 4 * (b - 1) + c + 1)
                        act.activation(QF[c], bank[c], ACT.Identity, bias=BC[:, c:c + 1]).then_inc(a["qf"], 1)
                        act.wait_ge(a["qf"], 4 * b + c + 1)
                        if b:
                            act.wait_ge(s_pb[c], 16 * b)
                        act.activation(PB[c][:, 0, :], QF[c], ACT.Copy).then_inc(a["h"], 1)
                act.wait_ge(s_const, 8 * 16)

            @block.vector
            def _(dve):
                t = Tally()

                def link(ins):
                    ins.then_inc(a["dve"], 1)
                    dve.wait_ge(a["dve"], t.step())

                dve.memset(ZI[:, :], 0).then_inc(a["init"], 1)
                dve.memset(ONE[:, :], 1.0).then_inc(a["one"], 1)
                dve.memset(MHALF[:, :], -0.5)
                dve.memset(MRUN[:, :], 0.0).then_inc(s["mrun"], 1)
                for p in range(2):
                    dve.memset(VA[p][:, :, :, :], 1.0)
                dve.wait_ge(s_rope, 48)
                for k in range(3):
                    even, odd = (WA[:, k, 0:2 * E].rearrange("p (q f two) -> p two q f", two=2, q=2)[:, n, :, :] for n in range(2))
                    reven, rodd = (WR[:, k, :].rearrange("p (q f two) -> p two q f", two=2, q=2)[:, n, :, :] for n in range(2))
                    cos, sin = (RT[:, n, :].unsqueeze(1).broadcast_to([P, 2, P]) for n in range(2))
                    tmp = [RTMP[:, n, :].rearrange("p (q f) -> p q f", q=2) for n in range(4)]
                    if k:
                        dve.wait_ge(a["wr"], k)
                    dve.tensor_tensor(tmp[0], even, cos, ALU.mult)
                    dve.tensor_tensor(tmp[1], odd, sin, ALU.mult)
                    dve.tensor_tensor(tmp[2], even, sin, ALU.mult)
                    link(dve.tensor_tensor(tmp[3], odd, cos, ALU.mult))
                    dve.tensor_tensor(reven, tmp[0], tmp[1], ALU.subtract)
                    dve.tensor_tensor(rodd, tmp[2], tmp[3], ALU.add).then_inc(a["wr"], 1)
                dve.wait_ge(a["bias"], 1)
                dve.tensor_copy(BC[:, :], MISC[:, 0:4]).then_inc(a["bc"], 1)

                def last_part(b, c):
                    dve.wait_ge(a["m"], 4 * b + c + 1)
                    dve.tensor_tensor(PB[c][:, 2, :], R1[c], PB[c][:, 1, :], ALU.subtract).then_inc(a["l"], 1)

                for b in range(B):
                    for c in range(4):
                        dve.wait_ge(a["h"], 4 * b + c + 1)
                        dve.tensor_tensor(R1[c], QF[c], PB[c][:, 0, :], ALU.subtract).then_inc(a["r"], 1)
                        if c:
                            last_part(b, c - 1)
                    for v in range(2):
                        dve.wait_ge(a["vps"], 2 * b + v + 1)
                        dve.tensor_tensor(VR[:, 4 * b + 2 * v:4 * b + 2 * v + 2, :],
                                          bank[4 + v].rearrange("p (n f) -> p n f", n=2),
                                          WA[:, 2, 2 * E:3 * E].unsqueeze(1).broadcast_to([P, 2, E]), ALU.add).then_inc(a["v"], 1)
                    last_part(b, 3)

            @block.tensor
            def _(pe):
                pe.wait_ge(a["wr"], 3)
                pe.wait_ge(a["one"], 1)
                for c in range(4):
                    last = nc.tensor.matmul(MISC[:, c:c + 1], WR[0:1, 2, c * P:(c + 1) * P], ONE[0:1, :], start=True, stop=True)
                last.then_inc(a["bias"], 1)
                for b in range(B):
                    pe.wait_ge(s_x[b], 16)
                    for c in range(4):
                        if b:
                            pe.wait_ge(a["qf"], 4 * (b - 1) + c + 1)
                        for k in range(KC):
                            last = nc.tensor.matmul(bank[c], WR[:, k, c * P:(c + 1) * P], XTB[b][:, k, :], start=(k == 0), stop=(k == KC - 1))
                        last.then_inc(a["ps"], 1)
                    for v in range(2):
                        if b:
                            pe.wait_ge(a["v"], 2 * (b - 1) + v + 1)
                        for n in range(2):
                            t0 = (2 * v + n) * P
                            for k in range(KC):
                                last = nc.tensor.matmul(bank[4 + v][:, n * E:(n + 1) * E], XTB[b][:, k, t0:t0 + P],
                                                        WA[:, k, 2 * E:3 * E], start=(k == 0), stop=(k == KC - 1))
                        last.then_inc(a["vps"], 1)

        def after(first, *waits):
            if not first:
                for eng, which, value in waits:
                    settle(eng, which, value)

        def settle(eng, which, value):
            if not isinstance(value, int):
                value = eng.to_reg(value)
                eng.wait_ge(which, 1)
            eng.wait_ge(which, value)

        def early(b, k, n):
            return isinstance(b, int) and b * NG + k < n

        with nc.Block() as block:
            @block.sync
            def _(sp):
                def load_unit(b, g):
                    u, p = b * NG + g, g % 2
                    after(early(b, g, 2), (sp, s["ST"], (u - 2) * NTG + NTG))
                    for which, dst, parts in ((1, K[p], KPART), (0, Q[p], QPART)):
                        for r, part in enumerate(parts):
                            src = qk_dram[which, part, g * GH * HD:(g + 1) * GH * HD, bass.ds(b * T, T)]
                            sp.dma_start(dst[r * HD:(r + 1) * HD, :, :], src.rearrange("(h d) t -> d h t", d=HD)).then_inc(s_kq[p], 16)

                def load_weights(b):
                    for n in range(NX // B):
                        e = b * (NX // B) + n
                        for k in range(KC):
                            sp.dma_start(W1[:, bass.ds((e + k * NX) * 2 * FF, 2 * FF)], w1T[:, bass.ds((e + k * NX) * 2 * FF, 2 * FF)]).then_inc(s_w, 16)
                        for k in range(FF // P):
                            sp.dma_start(W2[:, bass.ds((e + k * NX) * E, E)], w2T[:, bass.ds((e + k * NX) * E, E)]).then_inc(s_w, 16)

                def load_x(b):
                    after(early(b, 0, 1), (sp, s_x1w, b * 16))
                    sp.dma_start(XB[:, :, :], x[bass.ds(b * T, T), :].rearrange("(n p) f -> p n f", p=P)).then_inc(s_xb, 16)

                def store_x1(b):
                    sp.wait_ge(s["x1"], (b + 1) * TT)
                    sp.dma_start(x1_dram[bass.ds(b * T, T), :].rearrange("(n p) f -> p n f", p=P), X1[:, :, :]).then_inc(s_x1w, 16)

                for g in range(NG):
                    load_unit(0, g)
                load_x(0)
                load_weights(0)
                with sp.Fori(1, B) as b:
                    for g in range(NG):
                        load_unit(b, g)
                        if g == 0:
                            load_weights(b)
                    store_x1(b - 1)
                    load_x(b)
                store_x1(B - 1)
                sp.wait_ge(s_x1w, 16 * B)
                sp.wait_ge(s_w, 16 * NX * (KC + FF // P))

            @block.gpsimd
            def _(pool):
                t = Tally()

                def link(ins):
                    ins.then_inc(s["pool"], 1)
                    settle(pool, s["pool"], t.step())

                def fill_v(b, g):
                    u = b * NG + g
                    after(early(b, g, 2), (pool, s["pv"], (u - 2) * 3 + 3))
                    lo = HD * (g % 2)
                    for j in range(TT):
                        last = pool.tensor_copy(VA[g % 2][:, j, :, lo:lo + HD],
                                                VR[:, bass.ds(b * TT + j, 1), g * GH * HD:(g + 1) * GH * HD].rearrange("p o (h d) -> p (o h) d", d=HD))
                    last.then_inc(s["va"], 1)

                def maxima(b, g):
                    u, p = b * NG + g, g % 2
                    settle(pool, s["mx"], u + 1)
                    m = MX[p][:, :, 4:8].rearrange("p h i -> p i h")
                    part = [NP[p][:, :, r * GH:(r + 1) * GH] for r in range(PARTS)]
                    link(pool.tensor_scalar(NM[:, 0, :, :], m, -1.0, None, ALU.mult))
                    link(pool.tensor_copy(part[0], NM[:, 0, :, :]))
                    link(pool.tensor_tensor(NM[:, 1, :, :], NM[:, 0, :, :], part[0], ALU.subtract))
                    link(pool.tensor_copy(part[1], NM[:, 1, :, :]))
                    pool.tensor_tensor(part[2], NM[:, 1, :, :], part[1], ALU.subtract).then_inc(s["np"], 1)
                    settle(pool, s["np"], u + 1)

                def inverse_std(b):
                    for n in range(TT):
                        settle(pool, s["var"], b * TT + n + 1)
                        link(pool.tensor_scalar(VE[:, n, :], MV[:, n, 1:2], EPS, None, ALU.add))
                        pool.tensor_tensor(RS[:, n, :], VE[:, n, :], MHALF[:, :], ALU.pow).then_inc(s["rs"], 1)

                def residual(b):
                    settle(pool, s_xb, b * 16 + 16)
                    pool.tensor_tensor(XB[:, :, :], XB[:, :, :], BP[:, :].unsqueeze(1).broadcast_to([P, TT, E]), ALU.add).then_inc(s["xb"], 1)

                def scatter(b):
                    settle(pool, s["slots"], b + 1)
                    settle(pool, s_sc, b * (16 * TT * TOPK) + 16)
                    link(pool.tensor_copy(TOK4[:, :], TOK[:, bass.ds(b * TT, TT)]))
                    for n in range(TT):
                        for k in range(TOPK):
                            pool.indirect_dma_start(tok_dram, bass.IndirectOffsetOnAxis(ap=SLI[:, n, k:k + 1], axis=0),
                                                    TOK4[:, n:n + 1], None).then_inc(s_sc, 16)

                for g in range(NG):
                    fill_v(0, g)
                    maxima(0, g)
                residual(0)
                with pool.Fori(1, B) as b:
                    t.enter(b - 1, 4 * NG + TT + 1)
                    for g in range(NG):
                        fill_v(b, g)
                        if g == 2:
                            inverse_std(b - 1)
                        maxima(b, g)
                    scatter(b - 1)
                    residual(b)
                    t.leave(B - 1)
                inverse_std(B - 1)
                scatter(B - 1)
                settle(pool, s_sc, 16 * TT * TOPK * B + 16)

            def slot_of(k, n):
                return ((k - 1) * NTG + n) % 2

            @block.scalar
            def _(act):
                def exps(b, k):
                    v = b * NG + k - 1
                    for n in range(NTG):
                        act.wait_ge(s["ST"], v * NTG + n + 1)
                        after(early(b, k, 2), (act, s["pv"], (v - 1) * 3 + (1, 1, 2, 2, 3)[n]))
                        act.activation(PT[n][:, :], STb[slot_of(k, n)].rearrange("p a n -> p (a n)"), ACT.Exp).then_inc(s["exp"], 1)
                    act.wait_ge(s["pv"], v * 3 + 3)
                    after(early(b, k, 3), (act, s["rbm"], v - 1))
                    act.activation(O[(k - 1) % 2][:, :], Ob, ACT.Copy).then_inc(s["ocp"], 1)

                def gate_exp(b):
                    act.wait_ge(s["dl"], b + 1)
                    act.activation(EX[:, :], DL[:, :], ACT.Exp).then_inc(s["ex"], 1)

                def max_rows(b, k):
                    u, p = b * NG + k, k % 2
                    act.wait_ge(s["mt"], u + 1)
                    act.activation(Q[p][SK:SKM, :, :], miscb[SK:SKM, 0:T].unsqueeze(1).broadcast_to([PARTS * GH, GH, T]),
                                   ACT.Copy).then_inc(s["qm"], 1)

                max_rows(0, 0)
                for k in range(1, NG):
                    exps(0, k)
                    max_rows(0, k)
                with act.Fori(1, B) as b:
                    for k in range(NG):
                        exps(b, k)
                        max_rows(b, k)
                    gate_exp(b - 1)
                exps(B, 0)
                gate_exp(B - 1)

            @block.vector
            def _(dve):
                t = Tally()

                def link(ins):
                    ins.then_inc(s["dve"], 1)
                    settle(dve, s["dve"], t.step())

                def reduces(b, k, n):
                    u, p = b * NG + k, k % 2
                    dve.wait_ge(s["S"], u * NSG + n + 1)
                    if n == 0:
                        after(early(b, k, 2), (dve, s["np"], u - 1))
                    if n < 4:
                        ins = dve.tensor_reduce(MX[p][:, n, 7:8], Sb[n % 2], AX.X, ALU.max)
                    elif n < 8:
                        ins = dve.tensor_reduce(MX[p][:, n - 4, 1:5], Sb[n % 2].rearrange("p (a n) -> p a n", n=P), AX.X, ALU.max)
                    else:
                        h = 2 * (n - 8)
                        ins = dve.tensor_reduce(MX[p][:, h:h + 2, 5], Sb[n % 2].rearrange("p (a n) -> p a n", a=2), AX.X, ALU.max)
                    ins.then_inc(s["Sf"], 1)

                def maxima(b, k):
                    u, p = b * NG + k, k % 2
                    dve.wait_ge(s["Sf"], u * NSG + NSG)
                    dve.tensor_reduce(MX[p][:, :, 6], MX[p][:, :, 1:4], AX.X, ALU.max).then_inc(s["mx"], 1)

                def recip(b, k):
                    w = b * NG + k - 2
                    dve.wait_ge(s["ocp"], w + 1)
                    dve.reciprocal(RC[:, :], O[k % 2][:, :]).then_inc(s["rc"], 1)

                def normalise(b, k):
                    w, c = b * NG + k - 2, C[(k - 2) % 4 // 2]
                    dve.wait_ge(s["rb"], w + 1)
                    dst = TMP if k % 2 else c
                    dve.tensor_tensor(dst[:, :], bank[7], O[k % 2][:, :], ALU.mult).then_inc(s["rbm"], 1)
                    if k % 2:
                        dve.wait_ge(s["rbm"], w + 1)
                        dve.tensor_tensor(c[:, :], c[:, :], TMP[:, :], ALU.add).then_inc(s["pair"], 1)

                def post(b, n):
                    dve.wait_ge(s["ap"], b * TT + n + 1)
                    if n == 0:
                        dve.wait_ge(s["xb"], b + 1)
                    y = XB[:, n, :]
                    dve.tensor_tensor(y, bank[7][:, 0:E], y, ALU.add).then_inc(s["res"], 1)
                    dve.wait_ge(s["res"], b * TT + n + 1)
                    link(dve.bn_stats(ST6[:, n, :], y))
                    dve.bn_aggr(MV[:, n, :], ST6[:, n, :]).then_inc(s["var"], 1)

                def normal_row(b, n):
                    dve.wait_ge(s["rs"], b * TT + n + 1)
                    dve.tensor_scalar(X1[:, n, :], XB[:, n, :], MV[:, n, 0:1], RS[:, n, :], ALU.subtract, ALU.mult).then_inc(s["x1"], 1)

                def x1_columns(b, n):
                    dve.wait_ge(s["tp"], b * TT + n + 1)
                    dve.tensor_copy(XT1[:, n, :, :], bank[7][:, 0:KC * P].rearrange("p (k t) -> p k t", k=KC)).then_inc(s["xt"], 1)

                def top2(b):
                    dve.wait_ge(s["lgp"], b + 1)
                    dve.tensor_copy(LG[:, :, :], bank[7][:, 0:TT * NX].rearrange("p (n e) -> p n e", e=NX)).then_inc(s["lg"], 1)
                    settle(dve, s["lg"], b + 1)
                    for n in range(TT):
                        last = dve.max(MVX[:, n, :], LG[:, n, :])
                    link(last)
                    for n in range(TT):
                        last = dve.max_index(MIX[:, n, :], MVX[:, n, :], LG[:, n, :])
                    link(last)
                    dve.tensor_tensor(DL[:, :], MVX[:, :, 1], MVX[:, :, 0], ALU.subtract).then_inc(s["dl"], 1)
                    link(dve.tensor_copy(MIF[:, :, :], MIX[:, :, :]))
                    for k in range(TOPK):
                        last = dve.tensor_tensor(OH[k][:, :, :], iota8.unsqueeze(1).broadcast_to([P, TT, NX]),
                                                 MIF[:, :, k:k + 1].broadcast_to([P, TT, NX]), ALU.is_equal)
                    link(last)
                    dve.tensor_tensor(MC[:, :, :], OH[0][:, :, :], OH[1][:, :, :], ALU.add).then_inc(s["mc"], 1)

                def weights(b):
                    dve.wait_ge(s["ex"], b + 1)
                    link(dve.tensor_scalar(SM[:, :], EX[:, :], 1.0, None, ALU.add))
                    link(dve.reciprocal(WB4[:, :, 0], SM[:, :]))
                    link(dve.tensor_tensor(WB4[:, :, 1], WB4[:, :, 0], EX[:, :], ALU.mult))
                    link(dve.tensor_copy(WT[:, bass.ds(b * TT, TT), :], WB4[:, :, :]))

                def slots(b):
                    dve.wait_ge(s["rkp"], b + 1)
                    dve.tensor_tensor(RK[:, :, :], bank[7][:, 0:TT * NX].rearrange("p (n e) -> p n e", e=NX),
                                      ebase8.unsqueeze(1).broadcast_to([P, TT, NX]), ALU.add).then_inc(s["rk"], 1)
                    dve.wait_ge(s["rk"], b + 1)
                    for k in range(TOPK):
                        last = dve.tensor_tensor(RKO[k][:, :, :], RK[:, :, :], OH[k][:, :, :], ALU.mult)
                    link(last)
                    settle(dve, s_sc, b * (16 * TT * TOPK) + 16)
                    for k in range(TOPK):
                        last = dve.tensor_reduce(SLF[:, :, k], RKO[k][:, :, :], AX.X, ALU.add)
                    link(last)
                    dve.tensor_copy(SLI[:, :, :], SLF[:, :, :]).then_inc(s["slots"], 1)
                    link(dve.tensor_copy(SLR[:, bass.ds(b * TT * TOPK, TT * TOPK)], SLF[:, :, :].rearrange("p n k -> p (n k)")))
                    link(dve.tensor_reduce(MSUM[:, :], MC[:, :, :].rearrange("p n e -> p e n"), AX.X, ALU.add))
                    dve.tensor_tensor(MRUN[:, :], MRUN[:, :], MSUM[:, :], ALU.add).then_inc(s["mrun"], 1)
                    dve.wait_ge(s["mrun"], b + 2)

                def step(b, k, tails):
                    for n in range(NSG):
                        reduces(b, k, n)
                        if n == 1 and not early(b, k, 2):
                            recip(b, k)
                        if tails and k == 2 and 2 <= n < 6:
                            post(b - 1, n - 2)
                        if tails and k == 2 and 3 <= n < 7:
                            normal_row(b - 1, n - 3)
                        if tails and k == 2 and 6 <= n:
                            x1_columns(b - 1, n - 6)
                        if tails and k == 3 and n == 2:
                            top2(b - 1)
                        if tails and k == 3 and n == 7:
                            slots(b - 1)
                    maxima(b, k)
                    if not early(b, k, 2):
                        normalise(b, k)
                    if tails and k == 3:
                        weights(b - 1)

                for k in range(NG):
                    step(0, k, False)
                with dve.Fori(1, B) as b:
                    t.enter(b - 1, TT + 4 + 4 + 4)
                    for k in range(NG):
                        step(b, k, True)
                    t.leave(B - 1)
                for k in range(2):
                    recip(B, k)
                    normalise(B, k)
                for n in range(TT):
                    post(B - 1, n)
                    if n:
                        normal_row(B - 1, n - 1)
                normal_row(B - 1, TT - 1)
                for n in range(TT):
                    x1_columns(B - 1, n)
                top2(B - 1)
                slots(B - 1)
                weights(B - 1)
                dve.wait_ge(s["cnt"], 1)
                link(dve.tensor_copy(NF[:, :], bank[7][:, 0:NX]))
                link(dve.tensor_tensor(GE[:, :, :], NF[:, :].unsqueeze(2).broadcast_to([P, NX, 16]),
                                       thr16.unsqueeze(1).broadcast_to([P, NX, 16]), ALU.is_gt))
                link(dve.tensor_reduce(NT[:, :], GE[:, :, :], AX.X, ALU.add))
                link(dve.tensor_tensor(G8[:, :, :], tri8.rearrange("p (a b) -> p a b", a=NX),
                                       NT[:, :].unsqueeze(1).broadcast_to([P, NX, NX]), ALU.mult))
                link(dve.tensor_reduce(CT[:, :], G8[:, :, :], AX.X, ALU.add))
                link(dve.tensor_tensor(GJ[:, :, :], CT[0:1, :].unsqueeze(1).broadcast_to([1, NTAB, NX]),
                                       jidx[0:1, :].unsqueeze(2).broadcast_to([1, NTAB, NX]), ALU.is_le))
                link(dve.tensor_reduce(EJ[:, :], GJ[:, :, :], AX.X, ALU.add))
                link(dve.tensor_tensor(GP[:, :, :], GJ[:, :, :], NT[0:1, :].unsqueeze(1).broadcast_to([1, NTAB, NX]), ALU.mult))
                link(dve.tensor_reduce(PJ[:, :], GP[:, :, :], AX.X, ALU.add))
                link(dve.tensor_tensor(PJ[:, :], jidx[0:1, :], PJ[:, :], ALU.subtract))
                link(dve.tensor_scalar(PJ[:, :], PJ[:, :], float(P), None, ALU.mult))
                link(dve.scalar_tensor_tensor(RJ[:, :], EJ[:, :], float(REGION), PJ[:, :], ALU.mult, ALU.add))
                link(dve.tensor_copy(TAB[:, 0, :], RJ[:, :]))
                link(dve.tensor_scalar(TAB[:, 1, :], EJ[:, :], float(NX - 1), None, ALU.min))
                link(dve.tensor_scalar(SH[:, :], NT[:, 0:NX - 1], float(P), float(REGION), ALU.mult, ALU.subtract))
                wide = [P, NTT * TOPK, NX - 1]
                link(dve.tensor_tensor(GR[:, :, :], SLR[:, :].unsqueeze(2).broadcast_to(wide), ebase8[:, 1:NX].unsqueeze(1).broadcast_to(wide), ALU.is_ge))
                link(dve.tensor_tensor(GR2[:, :, :], GR[:, :, :], SH[:, :].unsqueeze(1).broadcast_to(wide), ALU.mult))
                link(dve.tensor_reduce(GR[:, :, 0], GR2[:, :, :], AX.X, ALU.add))
                link(dve.tensor_tensor(ROW[:, :], SLR[:, :], GR[:, :, 0], ALU.add))

            @block.tensor
            def _(pe):
                mm = nc.tensor.matmul

                def S(b, k, n):
                    u, p = b * NG + k, k % 2
                    if n == 0:
                        pe.wait_ge(s_kq[p], (b * 2 + k // 2 + 1) * (16 * 2 * len(QPART)))
                    after(early(b, k, 1) and n < 2, (pe, s["Sf"], u * NSG + n - 1))
                    dst = Sb[n % 2]

                    def tile_(h, i, at):
                        w = (i + 1) * P
                        mm(dst[:, at:at + w], Q[p][0:SK, h, i * P:(i + 1) * P], K[p][0:SK, h, 0:w], start=True, stop=False)
                        return mm(dst[:, at + w - P:at + w], identb, maskS, start=False, stop=True)

                    if n < 4:
                        last = tile_(n, 3, 0)
                    elif n < 8:
                        tile_(n - 4, 2, 0)
                        last = tile_(n - 4, 0, 3 * P)
                    else:
                        tile_(2 * (n - 8), 1, 0)
                        last = tile_(2 * (n - 8) + 1, 1, 2 * P)
                    last.then_inc(s["S"], 1)

                def where(h, j):
                    if j == 2:
                        return 4, h // 2, 2 * P * (h % 2)
                    return (0 if j == 0 else 2) + h // 2, h % 2, (0, 0, 0, 3 * P)[j]

                def ST(b, k, n):
                    v, p = b * NG + k - 1, (k - 1) % 2
                    if n == 0:
                        pe.wait_ge(s["qm"], v + 1)
                    after(early(b, k, 2) and n < 2, (pe, s["exp"], v * NTG + n - 1))
                    for h in range(GH):
                        for j in range(TT):
                            gr, bk, at = where(h, j)
                            if gr != n:
                                continue
                            dst = STb[slot_of(k, n)][:, bk, :]
                            mm(dst[:, at:at + T - j * P], K[p][0:SKM, h, j * P:(j + 1) * P], Q[p][0:SKM, h, j * P:T], start=True, stop=False)
                            last = mm(dst[:, at:at + P], identb, maskT, start=False, stop=True)
                    last.then_inc(s["ST"], 1)

                def PV(b, k, n):
                    v, p = b * NG + k - 1, (k - 1) % 2
                    pe.wait_ge(s["exp"], v * NTG + (2, 4, 5)[n])
                    if n == 0:
                        pe.wait_ge(s["va"], v + 1)
                        after(early(b, k, 2), (pe, s["ocp"], v))
                    for j in ((0,), (1, 3), (2,))[n]:
                        for h in range(GH):
                            gr, bk, at = where(h, j)
                            last = mm(Ob[32 * h:32 * h + 32, j * P:T], VA[p][:, j, h, :], PT[gr][:, bk * T + at:bk * T + at + T - j * P],
                                      start=(j == 0), stop=(j == 2), tile_position=(0, 32 * h))
                    last.then_inc(s["pv"], 1)

                def RB(b, k, last_reader):
                    w = b * NG + k - 2
                    pe.wait_ge(*last_reader)
                    pe.wait_ge(s["rc"], w + 1)
                    mm(bank[7], (selE, selO)[k % 2], RC[:, :], start=True, stop=True).then_inc(s["rb"], 1)

                def maxT(b, k, last_reader):
                    u, p = b * NG + k, k % 2
                    if last_reader:
                        pe.wait_ge(*last_reader)
                    pe.wait_ge(s["np"], u + 1)
                    for i in range(TT):
                        last = nc.tensor.transpose(miscb[SK:SKM, i * P:(i + 1) * P], NP[p][:, i, :], identb, tile_position=(0, SK))
                    last.then_inc(s["mt"], 1)

                def out_proj(b, n, last_reader):
                    pe.wait_ge(*last_reader)
                    if n == 0:
                        pe.wait_ge(s["pair"], b * 2 + 2)
                    for c in range(2):
                        last = mm(bank[7][:, 0:E], C[c][:, n * P:(n + 1) * P], WP[:, c, :], start=(c == 0), stop=(c == 1))
                    last.then_inc(s["ap"], 1)

                def x1_T(b, n, last_reader):
                    pe.wait_ge(*last_reader)
                    pe.wait_ge(s["x1"], b * TT + n + 1)
                    for k in range(KC):
                        last = nc.tensor.transpose(bank[7][:, k * P:(k + 1) * P], X1[:, n, k * P:(k + 1) * P], ident)
                    last.then_inc(s["tp"], 1)

                def logits(b, last_reader):
                    pe.wait_ge(*last_reader)
                    for n in range(TT):
                        for k in range(KC):
                            last = mm(bank[7][:, n * NX:(n + 1) * NX], XT1[:, n, k, :], RW[:, k, :], start=(k == 0), stop=(k == KC - 1))
                    last.then_inc(s["lgp"], 1)

                def ranks(b, last_reader):
                    pe.wait_ge(*last_reader)
                    pe.wait_ge(s["mc"], b + 1)
                    pe.wait_ge(s["mrun"], b + 1)
                    for n in range(TT):
                        dst = bank[7][:, n * NX:(n + 1) * NX]
                        mm(dst, tri, MC[:, n, :], start=True, stop=False)
                        for m in range(n):
                            mm(dst, onesb, MC[:, m, :], start=False, stop=False)
                        last = mm(dst, onesb, MRUN[:, :], start=False, stop=True)
                    last.then_inc(s["rkp"], 1)

                def step(b, k, tails):
                    u = b * NG + k
                    second = not early(b, k, 1)
                    reader = None if early(b, k, 1) else (s["qm"], u)
                    for n in range(NSG):
                        S(b, k, n)
                        if tails and k == 2:
                            if 2 <= n < 6:
                                out_proj(b - 1, n - 2, reader)
                                reader = (s["res"], (b - 1) * TT + n - 1)
                            elif n >= 6:
                                x1_T(b - 1, n - 6, reader)
                                reader = (s["xt"], (b - 1) * TT + n - 5)
                        if tails and k == 3 and n == 2:
                            logits(b - 1, reader)
                            reader = (s["lg"], b)
                        if tails and k == 3 and n == 7:
                            ranks(b - 1, reader)
                            reader = (s["rk"], b)
                        if second:
                            if n in (1, 2, 4, 6, 8):
                                ST(b, k, (1, 2, 4, 6, 8).index(n))
                            if n == 6:
                                PV(b, k, 0)
                            if n == 9:
                                PV(b, k, 1)
                    if not early(b, k, 2):
                        RB(b, k, reader)
                        reader = (s["rbm"], u - 1)
                    if second:
                        PV(b, k, 2)
                    maxT(b, k, reader)

                for k in range(NG):
                    step(0, k, False)
                with pe.Fori(1, B) as b:
                    for k in range(NG):
                        step(b, k, True)
                for n in range(NTG):
                    ST(B, 0, n)
                    if n == 1:
                        PV(B, 0, 0)
                    if n == 3:
                        PV(B, 0, 1)
                RB(B, 0, (s["qm"], NU))
                PV(B, 0, 2)
                RB(B, 1, (s["rbm"], NU - 1))
                reader = (s["rbm"], NU)
                for n in range(TT):
                    out_proj(B - 1, n, reader)
                    reader = (s["res"], (B - 1) * TT + n + 1)
                for n in range(TT):
                    x1_T(B - 1, n, reader)
                    reader = (s["xt"], (B - 1) * TT + n + 1)
                logits(B - 1, reader)
                ranks(B - 1, (s["lg"], B))
                pe.wait_ge(s["rk"], B)
                pe.wait_ge(s["mrun"], B + 1)
                mm(bank[7][:, 0:NX], onesb, MRUN[:, :], start=True, stop=True).then_inc(s["cnt"], 1)

        f = {n: sem("c_" + n) for n in ("xt", "xgt", "g", "u", "sil", "h", "th", "ht", "yp", "ys")}
        s_idx, s_g, s_yw = ([sem(f"s_{n}{q}") for q in range(TRIO)] for n in ("idx", "xg", "yw"))
        NTRIO = NTILES // TRIO
        G, U, XP, HP, YP = bank[0], bank[1], bank[2], bank[3], bank[4]

        with nc.Block() as block:
            @block.sync
            def _(sp):
                def first_slot(j):
                    return sp.value_load(TAB[0:1, 0, bass.ds(j, 1)], min_val=0, max_val=NSLOT - P)

                def fetch_tokens(i, q):
                    at = first_slot(i * TRIO + q)
                    sp.dma_start(IDX[q][:, :], tok_dram[bass.ds(at, P), :]).then_inc(s_idx[q], 16)

                for q in range(TRIO):
                    fetch_tokens(0, q)
                with sp.Fori(0, NTRIO) as i:
                    for q in range(TRIO):
                        sp.wait_ge(s_g[q], i * 16 + 16)
                        fetch_tokens(i + 1, q)
                        sp.wait_ge(f["ys"], i * TRIO + q + 1)
                        sp.dma_start(y_dram[bass.ds((i * TRIO + q) * P, P), :], YS[q]).then_inc(s_yw[q], 16)
                for q in range(TRIO):
                    sp.wait_ge(s_yw[q], 16 * NTRIO)

            @block.gpsimd
            def _(pool):
                def gather(i, q):
                    settle(pool, s_idx[q], i * 16 + 16)
                    pool.indirect_dma_start(XG[q], None, x1_dram, bass.IndirectOffsetOnAxis(ap=IDX[q][:, :], axis=0)).then_inc(s_g[q], 16)

                for q in range(TRIO):
                    gather(0, q)
                with pool.Fori(0, NTRIO) as i:
                    for q in range(TRIO):
                        settle(pool, f["xt"], i * TRIO + q + 1)
                        gather(i + 1, q)
                for q in range(TRIO):
                    settle(pool, s_g[q], 16 * (NTRIO + 1))

            @block.scalar
            def _(act):
                def columns(j):
                    act.wait_ge(f["xt"], j + 1)
                    act.activation(XGT.rearrange("p k t -> p (k t)"), XP[:, 0:E], ACT.Copy).then_inc(f["xgt"], 1)

                def silu(j):
                    act.wait_ge(f["g"], j + 1)
                    act.activation(SIL, G, ACT.Silu).then_inc(f["sil"], 1)

                def result(i, q, j):
                    act.wait_ge(f["yp"], j + 1)
                    after(isinstance(i, int) and i == 0, (act, s_yw[q], i * 16))
                    act.activation(YS[q], YP[:, 0:E], ACT.Copy).then_inc(f["ys"], 1)

                def tile_(i, q):
                    j = i * TRIO + q
                    silu(j)
                    if q:
                        result(i, q - 1, j - 1)
                    elif not (isinstance(i, int) and i == 0):
                        result(i - 1, TRIO - 1, j - 1)
                    columns(j + 1)

                columns(0)
                for i in range(2):
                    for q in range(TRIO):
                        tile_(i, q)
                with act.Fori(2, NTRIO) as i:
                    for q in range(TRIO):
                        tile_(i, q)
                result(NTRIO - 1, TRIO - 1, NTILES - 1)

            @block.vector
            def _(dve):
                def tile_(j):
                    dve.wait_ge(f["sil"], j + 1)
                    dve.wait_ge(f["u"], j + 1)
                    after(isinstance(j, int) and j == 0, (dve, f["th"], j))
                    dve.tensor_tensor(HH, U, SIL, ALU.mult).then_inc(f["h"], 1)
                    dve.wait_ge(f["th"], j + 1)
                    after(isinstance(j, int) and j == 0, (dve, f["yp"], j))
                    dve.tensor_copy(HT.rearrange("p k t -> p (k t)"), HP).then_inc(f["ht"], 1)

                tile_(0)
                with dve.Fori(1, NTILES) as j:
                    tile_(j)

            @block.tensor
            def _(pe):
                mm = nc.tensor.matmul

                def expert(j):
                    return pe.value_load(TAB[0:1, 1, bass.ds(j, 1)], min_val=0, max_val=NX - 1)

                def rows_T(i, q, j):
                    pe.wait_ge(s_g[q], i * 16 + 16)
                    after(isinstance(j, int) and j == 0, (pe, f["xgt"], j))
                    for k in range(KC):
                        last = nc.tensor.transpose(XP[:, k * P:(k + 1) * P], XG[q][:, k * P:(k + 1) * P], ident)
                    last.then_inc(f["xt"], 1)

                def up(j, e):
                    first = isinstance(j, int) and j == 0
                    pe.wait_ge(f["xgt"], j + 1)
                    for dst, n, done, used in ((G, 0, f["g"], f["sil"]), (U, 1, f["u"], f["h"])):
                        after(first, (pe, used, j))
                        for k in range(KC):
                            at = (e + k * NX) * (2 * FF) + n * FF
                            last = mm(dst, XGT[:, k, :], W1[:, bass.ds(at, FF)], start=(k == 0), stop=(k == KC - 1))
                        last.then_inc(done, 1)

                def hidden_T(j):
                    pe.wait_ge(f["h"], j + 1)
                    after(isinstance(j, int) and j == 0, (pe, f["ht"], j))
                    for k in range(FF // P):
                        last = nc.tensor.transpose(HP[:, k * P:(k + 1) * P], HH[:, k * P:(k + 1) * P], ident)
                    last.then_inc(f["th"], 1)

                def down(j, e):
                    pe.wait_ge(f["ht"], j + 1)
                    after(isinstance(j, int) and j == 0, (pe, f["ys"], j))
                    for k in range(FF // P):
                        last = mm(YP[:, 0:E], HT[:, k, :], W2[:, bass.ds((e + k * NX) * E, E)], start=(k == 0), stop=(k == FF // P - 1))
                    last.then_inc(f["yp"], 1)

                def trio(i):
                    e_before = None
                    for q in range(TRIO):
                        j = i * TRIO + q
                        e = expert(j)
                        up(j, e)
                        if q:
                            down(j - 1, e_before)
                        elif not isinstance(i, int):
                            down(j - 1, expert(j - 1))
                        if q < TRIO - 1:
                            rows_T(i, q + 1, j + 1)
                        else:
                            rows_T(i + 1, 0, j + 1)
                        hidden_T(j)
                        e_before = e

                rows_T(0, 0, 0)
                trio(0)
                with pe.Fori(1, NTRIO) as i:
                    trio(i)
                down(NTILES - 1, expert(NTILES - 1))

        d = {n: sem("d_" + n) for n in ("idx", "dve", "sum", "out", "pool", "var", "rs")}
        s_yg, s_xl, s_st = [sem(f"s_yg{n}") for n in range(TT)], sem("s_xl"), [sem(f"s_st{n}") for n in range(TT)]
        YG = [[PT[n][:, k * E:(k + 1) * E] for k in range(TOPK)] for n in range(TT)]
        OUT = [PT[n][:, 2 * E:3 * E] for n in range(TT)]
        XR = [XB, X1]

        with nc.Block() as block:
            @block.sync
            def _(sp):
                def load(b, dst):
                    after(early(b, 0, 1), (sp, d["out"], b * TT))
                    sp.dma_start(dst[:, :, :], x1_dram[bass.ds(b * T, T), :].rearrange("(n p) f -> p n f", p=P)).then_inc(s_xl, 16)

                load(0, X1)
                def store(b):
                    for n in range(TT):
                        sp.wait_ge(d["out"], b * TT + n + 1)
                        sp.dma_start(out[bass.ds(b * T + n * P, P), :], OUT[n]).then_inc(s_st[n], 16)

                store(0)
                with sp.Fori(1, B) as b:
                    load(b, X1)
                    store(b)
                for n in range(TT):
                    sp.wait_ge(s_st[n], 16 * B)

            @block.gpsimd
            def _(pool):
                def gather(b, first):
                    if not first:
                        for n in range(TT):
                            settle(pool, s_yg[n], b * 32)
                    pool.tensor_copy(IDG[:, :, :].rearrange("p n k -> p (n k)"), ROW[:, bass.ds(b * TT * TOPK, TT * TOPK)]).then_inc(d["idx"], 1)
                    settle(pool, d["idx"], b + 1)
                    for n in range(TT):
                        if not first:
                            settle(pool, d["sum"], (b - 1) * TT + n + 1)
                        for k in range(TOPK):
                            pool.indirect_dma_start(YG[n][k], None, y_dram, bass.IndirectOffsetOnAxis(ap=IDG[:, n, k:k + 1], axis=0)).then_inc(s_yg[n], 16)

                t = Tally()

                def inverse_std(b):
                    for n in range(TT):
                        settle(pool, d["var"], b * TT + n + 1)
                        pool.tensor_scalar(VE[:, n, :], MV[:, n, 1:2], EPS, None, ALU.add).then_inc(d["pool"], 1)
                        settle(pool, d["pool"], t.step())
                        pool.tensor_tensor(RS[:, n, :], VE[:, n, :], MHALF[:, :], ALU.pow).then_inc(d["rs"], 1)

                gather(0, True)
                inverse_std(0)
                with pool.Fori(1, B) as b:
                    t.enter(b - 1, TT)
                    gather(b, False)
                    inverse_std(b)
                    t.leave(B - 1)

            @block.vector
            def _(dve):
                t = Tally()

                def link(ins):
                    ins.then_inc(d["dve"], 1)
                    settle(dve, d["dve"], t.step())

                def tile_(b, n, first):
                    dve.wait_ge(s_xl, b * 16 + 16)
                    dve.wait_ge(s_yg[n], b * 32 + 32)
                    w = WT[:, bass.ds(b * TT + n, 1), :].rearrange("p o k -> p (o k)")
                    y = X1[:, n, :]
                    link(dve.scalar_tensor_tensor(y, YG[n][0], w[:, 0:1], y, ALU.mult, ALU.add))
                    dve.scalar_tensor_tensor(y, YG[n][1], w[:, 1:2], y, ALU.mult, ALU.add).then_inc(d["sum"], 1)
                    dve.wait_ge(d["sum"], b * TT + n + 1)
                    link(dve.bn_stats(ST6[:, n, :], y))
                    dve.bn_aggr(MV[:, n, :], ST6[:, n, :]).then_inc(d["var"], 1)

                def normal_row(b, n, first):
                    y = X1[:, n, :]
                    dve.wait_ge(d["rs"], b * TT + n + 1)
                    if not first:
                        dve.wait_ge(s_st[n], b * 16)
                    dve.tensor_scalar(OUT[n], y, MV[:, n, 0:1], RS[:, n, :], ALU.subtract, ALU.mult).then_inc(d["out"], 1)

                for n in range(TT):
                    tile_(0, n, True)
                for n in range(TT):
                    normal_row(0, n, True)
                with dve.Fori(1, B) as b:
                    t.enter(b - 1, 2 * TT)
                    for n in range(TT):
                        tile_(b, n, False)
                    for n in range(TT):
                        normal_row(b, n, False)
                    t.leave(B - 1)


def constants():
    f32 = np.float32
    cf = np.zeros((P, 480 + NTAB), f32)
    cf[:, 0:P] = np.eye(P)
    for j in range(GH):
        cf[32 * j + HD, P + 32 * j:P + 32 * j + HD] = E ** -0.5
        cf[32 * j, 2 * P + 32 * j + HD:2 * P + 32 * j + 2 * HD] = E ** -0.5
    cf[:, 384:392] = np.arange(NX)
    cf[:, 392:400] = np.arange(NX) * REGION
    cf[:, 400:416] = np.arange(16) * P
    cf[:, 416:480] = np.tril(np.ones((NX, NX))).reshape(-1)
    cf[:, 480:480 + NTAB] = np.arange(NTAB)
    bf = np.dtype("bfloat16")
    row, col = np.arange(P)[:, None], np.arange(P)[None, :]
    low = f32(-1e30)
    cb = np.concatenate([row == col, (col > row) * low, (row > col) * low, row < col, np.ones((P, P))], 1).astype(bf)
    kones = np.zeros((PARTS * GH, GH, T), bf)
    for r in range(PARTS):
        for h in range(GH):
            kones[r * GH + h, h, :] = 1
    freqs = f32(10000.0) ** (-(np.arange(0, HD, 2, dtype=f32) / f32(HD)))
    angle = np.outer(np.arange(H, dtype=f32), freqs).astype(f32).reshape(1, -1)
    cos_sin = np.concatenate([np.cos(angle), np.sin(angle)], 0).astype(f32)
    tokid = (np.arange(NTT)[None, :] * P + np.arange(P)[:, None]).astype(np.int32)
    return cf, cb, kones, cos_sin, tokid


def kernel(**inputs):
    import concourse.bacc as _bacc
    from concourse.bass_utils import run_bass_kernel_spmd as _run

    a = {k: np.asarray(v) for k, v in inputs.items()}
    x = a["L0_attn_x"].reshape(NTOK, E)
    wp = a["L0_attn_w_proj"].reshape(2, 2, GH, HD, E).transpose(0, 2, 1, 3, 4).reshape(2, P, E)
    cf, cb, kones, cos_sin, tokid = constants()
    arrays = {
        "x": x, "xT": x.T, "w_attn": a["L0_attn_w_attn"], "b_attn": a["L0_attn_b_attn"], "w_proj": wp,
        "b_proj": a["L0_attn_b_proj"], "router_wT": a["L0_ffn_router_w"].T,
        "w1T": a["L0_ffn_ws"].transpose(2, 0, 1).reshape(KC, P, NX, 2 * FF).transpose(1, 0, 2, 3).reshape(P, -1),
        "w2T": a["L0_ffn_w2s"].transpose(2, 0, 1).reshape(FF // P, P, NX, E).transpose(1, 0, 2, 3).reshape(P, -1),
        "cos_sin": cos_sin, "cf": cf, "cb": cb, "kones": kones, "tokid": tokid,
    }
    arrays = {k: np.ascontiguousarray(v) for k, v in arrays.items()}
    nc = _bacc.Bacc("TRN2", target_bir_lowering=False, num_devices=1)
    args = {k: nc.dram_tensor(k, v.shape, mybir.dt.from_np(v.dtype), kind="ExternalInput").ap() for k, v in arrays.items()}
    out = nc.dram_tensor("out", (NTOK, E), F32, kind="ExternalOutput").ap()
    block_kernel(nc, out=out, **args)
    r = _run(nc, [arrays], core_ids=[0])
    return r.results[0]["out"].reshape(B, T, E)
```

```python
import concourse.bass as bass
from concourse import mybir
from contextlib import ExitStack
import numpy as np

F32 = mybir.dt.float32
BF16 = mybir.dt.bfloat16
I32 = mybir.dt.int32
U32 = mybir.dt.uint32
ALU = mybir.AluOpType
ACT = mybir.ActivationFunctionType
AX = mybir.AxisListType

P = 128
B, T, E = 4, 512, 256
H, HD = 16, 16
NTOK = B * T
NTT = NTOK // P
TT = T // P
KC = E // P
NG = 4
GH = H // NG
NU = B * NG
PARTS = 3
QPART = [0, 0, 0, 1, 1, 2]
KPART = [0, 1, 2, 0, 1, 0]
SK = HD * len(QPART)
SKM = SK + PARTS * GH
NX, FF, TOPK = 8, 512, 2
REGION = NTOK
NTILES = NTOK * TOPK // P + NX - 1
TRIO = 3
NTAB = NTILES + TRIO
NSLOT = NX * REGION + NTAB * P
EPS = 1e-5
NSG, NTG = 10, 5


class Tally:

    def __init__(self):
        self.base, self.n = 0, 0

    def step(self):
        self.n += 1
        return self.base + self.n

    def enter(self, trip, per):
        self.start, self.per, self.n = self.base + self.n, per, 0
        self.base = trip * per + self.start

    def leave(self, trips):
        assert self.n == self.per, (self.n, self.per)
        self.base, self.n = self.start + trips * self.per, 0


def block_kernel(nc, x, xT, w_attn, b_attn, w_proj, b_proj, router_wT, w1T, w2T, cos_sin, cf, cb, kones, tokid, out):
    ctx = ExitStack()
    with ctx:
        def sb(name, shape, dt=F32):
            return ctx.enter_context(nc.sbuf_tensor(name, shape, dt))

        def sem(name):
            return ctx.enter_context(nc.semaphore(name))

        def dram(name, shape, dt):
            return nc.dram_tensor(name, shape, dt, kind="Internal").ap()

        qk_dram = dram("qk_parts", (2, PARTS, E, NTOK), BF16)
        x1_dram = dram("x1_rows", (NTOK, E), F32)
        tok_dram = dram("slot_token", (NSLOT, 1), I32)
        y_dram = dram("tile_out", (NTILES * P, E), F32)

        W1 = sb("W1", [P, KC * NX * 2 * FF])
        W2 = sb("W2", [P, 4 * NX * E])
        w1 = W1[:, :].rearrange("p (k e f) -> p k e f", k=KC, e=NX)
        w2 = W2[:, :].rearrange("p (k e f) -> p k e f", k=4, e=NX)
        CF = sb("CF", [P, cf.shape[1]])
        ident = CF[:, 0:P]
        iota8, ebase8 = CF[:, 128:136], CF[:, 136:144]
        thr16, tri8, jidx = CF[:, 144:160], CF[:, 160:224], CF[:, 224:224 + NTAB]
        CB = sb("CB", [P, 5 * P], BF16)
        identb, maskS, maskT, tri, onesb = (CB[:, n * P:(n + 1) * P] for n in range(5))
        WP = sb("WP", [P, 2, E])
        RW = sb("RW", [P, KC, NX])
        BP = sb("BP", [P, E])
        VR = sb("VR", [P, NTT, E])
        X1 = sb("X1", [P, TT, E])
        WT = sb("WT", [P, NTT, TOPK])
        SLR = sb("SLR", [P, NTT * TOPK])
        ROW = sb("ROW", [P, NTT * TOPK], I32)
        GR = sb("GR", [P, NTT * TOPK, NX - 1])
        GR2 = sb("GR2", [P, NTT * TOPK, NX - 1])
        SH = sb("SH", [P, NX - 1])
        TOK = sb("TOK", [P, NTT], I32)
        TAB = sb("TAB", [1, 2, NTAB], I32)
        K = [sb(f"K{g}", [P, GH, T], BF16) for g in range(NG)]
        Q = [sb(f"Q{g}", [P, GH, T], BF16) for g in range(NG)]
        VA = [sb(f"VA{p}", [P, TT, GH, 2 * HD]) for p in range(2)]
        O = sb("O", [P, T])
        PT = [sb(f"PT{n}", [P, 2 * T]) for n in range(NTG)]
        RC = sb("RC", [P, TT, GH, 1])
        AO = sb("AO", [P, TT, E])
        MX = [sb(f"MX{p}", [P, GH, 8]) for p in range(2)]
        NM = sb("NM", [P, 2, TT, GH])
        NP = [sb(f"NP{p}", [P, TT, PARTS * GH], BF16) for p in range(2)]
        XB = sb("XB", [P, TT, E])
        ST6 = sb("ST6", [P, TT, 6])
        MV = sb("MV", [P, TT, 2])
        VE = sb("VE", [P, TT, 1])
        RS = sb("RS", [P, TT, 1])
        MHALF = sb("MHALF", [P, 1])
        XT1 = sb("XT1", [P, TT, KC, P])
        LG = sb("LG", [P, TT, NX])
        MVX = sb("MVX", [P, TT, 8])
        MIX = sb("MIX", [P, TT, 8], U32)
        MIF = sb("MIF", [P, TT, 8])
        OH = [sb(f"OH{k}", [P, TT, NX]) for k in range(TOPK)]
        MC = sb("MC", [P, TT, NX], BF16)
        MRUN = sb("MRUN", [P, NX], BF16)
        MSUM = sb("MSUM", [P, NX])
        DL = sb("DL", [P, TT])
        EX = sb("EX", [P, TT])
        SM = sb("SM", [P, TT])
        RK = sb("RK", [P, TT, NX])
        RKO = [sb(f"RKO{k}", [P, TT, NX]) for k in range(TOPK)]
        SLF = sb("SLF", [P, TT, TOPK])
        SLI = sb("SLI", [P, TT, TOPK], I32)
        TOK4 = sb("TOK4", [P, TT], I32)
        WB4 = sb("WB4", [P, TT, TOPK])
        WA = W1[:, 0:2304].rearrange("p (k f) -> p k f", k=3)
        WR = W1[:, 2304:3840].rearrange("p (k f) -> p k f", k=3)
        RT = W1[:, 3840:4096].rearrange("p (k f) -> p k f", k=2)
        RTMP = W1[:, 4096:5120].rearrange("p (k f) -> p k f", k=4)
        XTB = [W1[:, 5120 + 1024 * n:6144 + 1024 * n].rearrange("p (k t) -> p k t", k=KC) for n in range(B)]
        QF = [W1[:, 9216 + 512 * n:9728 + 512 * n] for n in range(4)]
        R1 = [W1[:, 11264 + 512 * n:11776 + 512 * n] for n in range(4)]
        PB = [W1[:, 13312 + 768 * n:14080 + 768 * n].bitcast(BF16).rearrange("p (r t) -> p r t", r=3) for n in range(4)]
        BC = sb("BC", [P, 4])
        ONE = sb("ONE", [P, 1])
        XG = [PT[0][:, 256 * n:256 * n + 256] for n in range(3)]
        XGT = PT[1][:, 0:256].rearrange("p (k t) -> p k t", k=KC)
        SIL, HH = PT[2][:, 0:512], PT[2][:, 512:1024]
        HT = PT[3][:, 0:512].rearrange("p (k t) -> p k t", k=4)
        YS = [PT[4][:, 256 * n:256 * n + 256] for n in range(3)]
        IDX = [sb(f"IDX{n}", [P, 1], I32) for n in range(3)]
        IDG = sb("IDG", [P, TT, TOPK], I32)
        ZI = sb("ZI", [P, NSLOT // P], I32)
        NF = sb("NF", [P, NX])
        GE = sb("GE", [P, NX, 16])
        NT = sb("NT", [P, NX])
        CT = sb("CT", [P, NX])
        G8 = sb("G8", [P, NX, NX])
        GJ = sb("GJ", [1, NTAB, NX])
        GP = sb("GP", [1, NTAB, NX])
        EJ = sb("EJ", [1, NTAB])
        PJ = sb("PJ", [1, NTAB])
        RJ = sb("RJ", [1, NTAB])

        PS = ctx.enter_context(nc.psum_tensor("PS", [P, 8, 512], F32))
        bank = [PS[:, n, :] for n in range(8)]
        Sb = [bank[0], bank[1]]
        STb = [PS[:, 2 + 2 * n:4 + 2 * n, :] for n in range(2)]
        Ob = bank[6]
        Ot = Ob.rearrange("p (i h d) -> p i h d", i=TT, h=GH)
        MISC = bank[7]
        LEFT, RIGHT = MISC[:, 0:E], MISC[:, E:2 * E]
        miscb = MISC.bitcast(BF16)

        s_const, s_rope, s_x = sem("s_const"), sem("s_rope"), [sem(f"s_x{b}") for b in range(B)]
        s_sync = {n: sem("a_" + n) for n in ("init", "one", "dve", "wr", "bias", "bc", "ps", "vps", "qf", "h", "r", "m", "l", "v")}
        a = s_sync
        s_pb = [sem(f"s_pb{c}") for c in range(4)]

        names = ("S", "Sf", "mx", "np", "pool", "qm", "ST", "exp", "pv", "va", "ocp", "ot", "rc", "nrm",
                 "mt", "at", "atc", "ap", "res", "x1", "xb", "tp", "xt", "lgp", "lg", "mc", "rkp", "rk", "mrun", "dve", "dl", "ex", "slots",
                 "cnt", "var", "rs")
        s = {n: sem("b_" + n) for n in names}
        s_kq = [sem(f"s_kq{g}") for g in range(NG)]
        s_xb, s_x1w, s_w, s_sc = sem("s_xb"), sem("s_x1w"), sem("s_w"), sem("s_sc")

        with nc.Block() as block:
            @block.sync
            def _(sp):
                sp.dma_start(WA[:, 0:2, :], w_attn.rearrange("(k p) f -> p k f", p=P)).then_inc(s_rope, 16)
                sp.dma_start(WA[:, 2, :], b_attn.partition_broadcast(P)).then_inc(s_rope, 16)
                sp.dma_start(RT, cos_sin.partition_broadcast(P)).then_inc(s_rope, 16)
                for b in range(B):
                    sp.dma_start(XTB[b], xT[:, b * T:(b + 1) * T].rearrange("(k p) t -> p k t", p=P)).then_inc(s_x[b], 16)
                for b in range(B):
                    for c in range(4):
                        sp.wait_ge(a["l"], 4 * b + c + 1)
                        sp.dma_start(qk_dram[c // 2, :, (c % 2) * P:(c % 2 + 1) * P, b * T:(b + 1) * T].rearrange("r p t -> p r t"),
                                     PB[c]).then_inc(s_pb[c], 16)
                for c in range(4):
                    sp.wait_ge(s_pb[c], 16 * B)

            @block.gpsimd
            def _(pool):
                pool.wait_ge(a["init"], 1)
                pool.dma_start(tok_dram.rearrange("(p n) o -> p (n o)", p=P), ZI[:, :]).then_inc(s_sc, 16)
                for b in range(B):
                    for c in range(4):
                        pool.wait_ge(a["r"], 4 * b + c + 1)
                        pool.tensor_copy(PB[c][:, 1, :], R1[c]).then_inc(a["m"], 1)
                pool.wait_ge(s_sc, 16)

            @block.scalar
            def _(act):
                act.dma_start(CF[:, :], cf).then_inc(s_const, 16)
                act.dma_start(CB[:, :], cb).then_inc(s_const, 16)
                for g in range(NG):
                    act.dma_start(K[g][SK:SKM, :, :], kones).then_inc(s_const, 16)
                act.dma_start(WP[:, :, :], w_proj.rearrange("c p f -> p c f")).then_inc(s_const, 16)
                act.dma_start(RW[:, :, :], router_wT.rearrange("(k p) e -> p k e", p=P)).then_inc(s_const, 16)
                act.dma_start(BP[:, :], b_proj.partition_broadcast(P)).then_inc(s_const, 16)
                act.dma_start(TOK[:, :], tokid).then_inc(s_const, 16)
                act.wait_ge(a["bc"], 1)
                for b in range(B):
                    for c in range(4):
                        act.wait_ge(a["ps"], 4 * b + c + 1)
                        if b:
                            act.wait_ge(a["l"], 4 * (b - 1) + c + 1)
                        act.activation(QF[c], bank[c], ACT.Identity, bias=BC[:, c:c + 1]).then_inc(a["qf"], 1)
                        act.wait_ge(a["qf"], 4 * b + c + 1)
                        if b:
                            act.wait_ge(s_pb[c], 16 * b)
                        act.activation(PB[c][:, 0, :], QF[c], ACT.Copy).then_inc(a["h"], 1)
                act.wait_ge(s_const, 10 * 16)

            @block.vector
            def _(dve):
                t = Tally()

                def link(ins):
                    ins.then_inc(a["dve"], 1)
                    dve.wait_ge(a["dve"], t.step())

                dve.memset(ZI[:, :], 0).then_inc(a["init"], 1)
                dve.memset(ONE[:, :], 1.0).then_inc(a["one"], 1)
                dve.memset(MHALF[:, :], -0.5)
                dve.memset(MRUN[:, :], 0.0).then_inc(s["mrun"], 1)
                for p in range(2):
                    dve.memset(VA[p][:, :, :, :], float(E) ** 0.5)
                dve.wait_ge(s_rope, 48)
                for k in range(3):
                    even, odd = (WA[:, k, 0:2 * E].rearrange("p (q f two) -> p two q f", two=2, q=2)[:, n, :, :] for n in range(2))
                    reven, rodd = (WR[:, k, :].rearrange("p (q f two) -> p two q f", two=2, q=2)[:, n, :, :] for n in range(2))
                    cos, sin = (RT[:, n, :].unsqueeze(1).broadcast_to([P, 2, P]) for n in range(2))
                    tmp = [RTMP[:, n, :].rearrange("p (q f) -> p q f", q=2) for n in range(4)]
                    if k:
                        dve.wait_ge(a["wr"], k)
                    dve.tensor_tensor(tmp[0], even, cos, ALU.mult)
                    dve.tensor_tensor(tmp[1], odd, sin, ALU.mult)
                    dve.tensor_tensor(tmp[2], even, sin, ALU.mult)
                    link(dve.tensor_tensor(tmp[3], odd, cos, ALU.mult))
                    dve.tensor_tensor(reven, tmp[0], tmp[1], ALU.subtract)
                    dve.tensor_tensor(rodd, tmp[2], tmp[3], ALU.add).then_inc(a["wr"], 1)
                dve.wait_ge(a["bias"], 1)
                dve.tensor_copy(BC[:, :], MISC[:, 0:4]).then_inc(a["bc"], 1)

                def last_part(b, c):
                    dve.wait_ge(a["m"], 4 * b + c + 1)
                    dve.tensor_tensor(PB[c][:, 2, :], R1[c], PB[c][:, 1, :], ALU.subtract).then_inc(a["l"], 1)

                for b in range(B):
                    for c in range(4):
                        dve.wait_ge(a["h"], 4 * b + c + 1)
                        dve.tensor_tensor(R1[c], QF[c], PB[c][:, 0, :], ALU.subtract).then_inc(a["r"], 1)
                        if c:
                            last_part(b, c - 1)
                    for v in range(2):
                        dve.wait_ge(a["vps"], 2 * b + v + 1)
                        dve.tensor_tensor(VR[:, 4 * b + 2 * v:4 * b + 2 * v + 2, :],
                                          bank[4 + v].rearrange("p (n f) -> p n f", n=2),
                                          WA[:, 2, 2 * E:3 * E].unsqueeze(1).broadcast_to([P, 2, E]), ALU.add).then_inc(a["v"], 1)
                    last_part(b, 3)

            @block.tensor
            def _(pe):
                pe.wait_ge(a["wr"], 3)
                pe.wait_ge(a["one"], 1)
                for c in range(4):
                    last = nc.tensor.matmul(MISC[:, c:c + 1], WR[0:1, 2, c * P:(c + 1) * P], ONE[0:1, :], start=True, stop=True)
                last.then_inc(a["bias"], 1)
                for b in range(B):
                    pe.wait_ge(s_x[b], 16)
                    for c in range(4):
                        if b:
                            pe.wait_ge(a["qf"], 4 * (b - 1) + c + 1)
                        for k in range(KC):
                            last = nc.tensor.matmul(bank[c], WR[:, k, c * P:(c + 1) * P], XTB[b][:, k, :], start=(k == 0), stop=(k == KC - 1))
                        last.then_inc(a["ps"], 1)
                    for v in range(2):
                        if b:
                            pe.wait_ge(a["v"], 2 * (b - 1) + v + 1)
                        for n in range(2):
                            t0 = (2 * v + n) * P
                            for k in range(KC):
                                last = nc.tensor.matmul(bank[4 + v][:, n * E:(n + 1) * E], XTB[b][:, k, t0:t0 + P],
                                                        WA[:, k, 2 * E:3 * E], start=(k == 0), stop=(k == KC - 1))
                        last.then_inc(a["vps"], 1)

        def after(first, *waits):
            if not first:
                for eng, which, value in waits:
                    settle(eng, which, value)

        def settle(eng, which, value):
            if not isinstance(value, int):
                value = eng.to_reg(value)
                eng.wait_ge(which, 1)
            eng.wait_ge(which, value)

        def early(b, k, n):
            return isinstance(b, int) and b * NG + k < n

        with nc.Block() as block:
            @block.sync
            def _(sp):
                def load_unit(b, g):
                    u = b * NG + g
                    after(early(b, g, NG), (sp, s["ST"], (u - NG) * NTG + NTG))
                    for which, dst, parts in ((1, K[g], KPART), (0, Q[g], QPART)):
                        for r, part in enumerate(parts):
                            src = qk_dram[which, part, g * GH * HD:(g + 1) * GH * HD, bass.ds(b * T, T)]
                            sp.dma_start(dst[r * HD:(r + 1) * HD, :, :], src.rearrange("(h d) t -> d h t", d=HD)).then_inc(s_kq[g], 16)

                def load_weights(b):
                    for n in range(NX // B):
                        e = b * (NX // B) + n
                        for k in range(KC):
                            sp.dma_start(W1[:, bass.ds((e + k * NX) * 2 * FF, 2 * FF)], w1T[:, bass.ds((e + k * NX) * 2 * FF, 2 * FF)]).then_inc(s_w, 16)
                        for k in range(FF // P):
                            sp.dma_start(W2[:, bass.ds((e + k * NX) * E, E)], w2T[:, bass.ds((e + k * NX) * E, E)]).then_inc(s_w, 16)

                for g in range(NG):
                    load_unit(0, g)
                sp.dma_start(XB[:, :, :], x[0:T, :].rearrange("(n p) f -> p n f", p=P)).then_inc(s_xb, 16)
                load_weights(0)
                with sp.Fori(1, B) as b:
                    for g in range(NG):
                        load_unit(b, g)
                    load_weights(b)
                sp.wait_ge(s_w, 16 * NX * (KC + FF // P))

            @block.gpsimd
            def _(pool):
                t = Tally()

                def link(ins):
                    ins.then_inc(s["pool"], 1)
                    settle(pool, s["pool"], t.step())

                def fill_v(b, k):
                    v, g = b * NG + k - 1, (k - 1) % NG
                    row = b if k else b - 1
                    after(early(b, k, 3), (pool, s["pv"], (v - 2) * 3 + 3))
                    for j in range(TT):
                        last = pool.tensor_copy(VA[g % 2][:, j, :, 0:HD],
                                                VR[:, bass.ds(row * TT + j, 1), g * GH * HD:(g + 1) * GH * HD].rearrange("p o (h d) -> p (o h) d", d=HD))
                    last.then_inc(s["va"], 1)

                def maxima(b, g):
                    u, p = b * NG + g, g % 2
                    settle(pool, s["mx"], u + 1)
                    m = MX[p][:, :, 4:8].rearrange("p h i -> p i h")
                    part = [NP[p][:, :, r * GH:(r + 1) * GH] for r in range(PARTS)]
                    link(pool.tensor_scalar(NM[:, 0, :, :], m, -1.0, None, ALU.mult))
                    link(pool.tensor_copy(part[0], NM[:, 0, :, :]))
                    link(pool.tensor_tensor(NM[:, 1, :, :], NM[:, 0, :, :], part[0], ALU.subtract))
                    link(pool.tensor_copy(part[1], NM[:, 1, :, :]))
                    pool.tensor_tensor(part[2], NM[:, 1, :, :], part[1], ALU.subtract).then_inc(s["np"], 1)
                    settle(pool, s["np"], u + 1)

                def inverse_std(b, n):
                    settle(pool, s["var"], b * TT + n + 1)
                    link(pool.tensor_scalar(VE[:, n, :], MV[:, n, 1:2], EPS, None, ALU.add))
                    pool.tensor_tensor(RS[:, n, :], VE[:, n, :], MHALF[:, :], ALU.pow).then_inc(s["rs"], 1)

                def residual(b):
                    after(early(b, 0, 1), (pool, s_x1w, b * 16))
                    settle(pool, s_xb, b * 16 + 16)
                    pool.tensor_tensor(XB[:, :, :], XB[:, :, :], BP[:, :].unsqueeze(1).broadcast_to([P, TT, E]), ALU.add).then_inc(s["xb"], 1)

                def scatter(b):
                    settle(pool, s["slots"], b + 1)
                    settle(pool, s_sc, b * (16 * TT * TOPK) + 16)
                    link(pool.tensor_copy(TOK4[:, :], TOK[:, bass.ds(b * TT, TT)]))
                    for n in range(TT):
                        for k in range(TOPK):
                            pool.indirect_dma_start(tok_dram, bass.IndirectOffsetOnAxis(ap=SLI[:, n, k:k + 1], axis=0),
                                                    TOK4[:, n:n + 1], None).then_inc(s_sc, 16)

                for g in range(NG):
                    if g:
                        fill_v(0, g)
                    maxima(0, g)
                residual(0)
                with pool.Fori(1, B) as b:
                    t.enter(b - 1, 4 * NG + TT + 1)
                    for g in range(NG):
                        fill_v(b, g)
                        if g >= 2:
                            for n in range(2 * g - 4, 2 * g - 2):
                                inverse_std(b - 1, n)
                        maxima(b, g)
                    scatter(b - 1)
                    residual(b)
                    t.leave(B - 1)
                fill_v(B, 0)
                for n in range(TT):
                    inverse_std(B - 1, n)
                scatter(B - 1)
                settle(pool, s_sc, 16 * TT * TOPK * B + 16)

            ST_AT = {0: 0, 2: 1, 4: 2, 6: 3, 8: 4}
            PV_AT = {1: 2, 7: 0, 9: 1}
            OT_AT = 3
            MAXT_AT = (4, 4, 4, 7)
            AT_AT = {(2, 5): 0, (2, 7): 1, (2, 9): 2, (3, 1): 3}
            OUT_AT = {(2, 6): 0, (2, 8): 1, (3, 0): 2, (3, 2): 3}
            POST_AT = {(2, 7): 0, (2, 9): 1, (3, 1): 2, (3, 3): 3}
            NORM_AT = {(2, 9): 0, (3, 1): 1, (3, 2): 2, (3, 4): 3}
            XT_AT = {(3, 4): 0, (3, 5): 1, (3, 6): 2, (3, 7): 3}
            LOGITS_AT, TOP2_AT, RANKS_AT = (3, 8), (3, 8), (3, 9)

            def slot_of(k, n):
                return (k * NTG + n) % 2

            @block.scalar
            def _(act):
                def exps(b, k, n):
                    v = b * NG + k - 2
                    act.wait_ge(s["ST"], v * NTG + n + 1)
                    after(early(b, k, 3), (act, s["pv"], (v - 1) * 3 + (1, 1, 2, 2, 3)[n]))
                    act.activation(PT[n][:, :], STb[slot_of(k, n)].rearrange("p a n -> p (a n)"), ACT.Exp).then_inc(s["exp"], 1)

                def outputs(b, k):
                    act.wait_ge(s["pv"], (b * NG + k - 3) * 3 + 3)
                    act.activation(O[:, :], Ob, ACT.Copy).then_inc(s["ocp"], 1)

                def ao_columns(b, n):
                    act.wait_ge(s["at"], b * TT + n + 1)
                    act.activation(XT1[:, n, :, :].rearrange("p k t -> p (k t)"), LEFT, ACT.Copy).then_inc(s["atc"], 1)

                def x1_columns(b, n):
                    act.wait_ge(s["tp"], b * TT + n + 1)
                    act.activation(XT1[:, n, :, :].rearrange("p k t -> p (k t)"), LEFT, ACT.Copy).then_inc(s["xt"], 1)

                def gate_exp(b):
                    act.wait_ge(s["dl"], b + 1)
                    act.activation(EX[:, :], DL[:, :], ACT.Exp).then_inc(s["ex"], 1)

                def max_rows(b, k):
                    u, g = b * NG + k, (k - 1) % NG
                    act.wait_ge(s["mt"], u)
                    act.activation(Q[g][SK:SKM, :, :], miscb[SK:SKM, 0:T].unsqueeze(1).broadcast_to([PARTS * GH, GH, T]),
                                   ACT.Copy).then_inc(s["qm"], 1)

                def step(b, k, tails):
                    for n in range(NSG):
                        if n in ST_AT and not early(b, k, 2):
                            exps(b, k, ST_AT[n])
                        if n == 1 and not early(b, k, 3):
                            outputs(b, k)
                        if tails and (k, n) in AT_AT:
                            ao_columns(b - 1, AT_AT[k, n])
                        if tails and (k, n) in XT_AT:
                            x1_columns(b - 1, XT_AT[k, n])
                        if n == MAXT_AT[k] and not early(b, k, 1):
                            max_rows(b, k)
                    if tails and k == 3:
                        gate_exp(b - 1)
                        act.wait_ge(s["x1"], b * TT)
                        act.dma_start(x1_dram[bass.ds((b - 1) * T, T), :].rearrange("(n p) f -> p n f", p=P), X1[:, :, :]).then_inc(s_x1w, 16)
                        act.dma_start(XB[:, :, :], x[bass.ds(b * T, T), :].rearrange("(n p) f -> p n f", p=P)).then_inc(s_xb, 16)

                for k in range(NG):
                    step(0, k, False)
                with act.Fori(1, B) as b:
                    for k in range(NG):
                        step(b, k, True)
                for k in range(2):
                    for n in range(NTG):
                        exps(B, k, n)
                        if n == 0:
                            outputs(B, k)
                    if k == 0:
                        max_rows(B, 0)
                outputs(B, 2)
                for n in range(TT):
                    ao_columns(B - 1, n)
                for n in range(TT):
                    x1_columns(B - 1, n)
                act.dma_start(x1_dram[(B - 1) * T:B * T, :].rearrange("(n p) f -> p n f", p=P), X1[:, :, :]).then_inc(s_x1w, 16)
                gate_exp(B - 1)
                act.wait_ge(s_x1w, 16 * B)

            @block.vector
            def _(dve):
                t = Tally()

                def link(ins):
                    ins.then_inc(s["dve"], 1)
                    settle(dve, s["dve"], t.step())

                def reduces(b, k, n):
                    u, p = b * NG + k, k % 2
                    dve.wait_ge(s["S"], u * NSG + n + 1)
                    if n == 0:
                        after(early(b, k, 2), (dve, s["np"], u - 1))
                    if n < 4:
                        ins = dve.tensor_reduce(MX[p][:, n, 7:8], Sb[n % 2], AX.X, ALU.max)
                    elif n < 8:
                        ins = dve.tensor_reduce(MX[p][:, n - 4, 1:5], Sb[n % 2].rearrange("p (a n) -> p a n", n=P), AX.X, ALU.max)
                    else:
                        h = 2 * (n - 8)
                        ins = dve.tensor_reduce(MX[p][:, h:h + 2, 5], Sb[n % 2].rearrange("p (a n) -> p a n", a=2), AX.X, ALU.max)
                    ins.then_inc(s["Sf"], 1)

                def maxima(b, k):
                    u, p = b * NG + k, k % 2
                    dve.wait_ge(s["Sf"], u * NSG + NSG)
                    dve.tensor_reduce(MX[p][:, :, 6], MX[p][:, :, 1:4], AX.X, ALU.max).then_inc(s["mx"], 1)

                def normalise(b, k):
                    w, g = b * NG + k - 3, (k - 3) % NG
                    dve.wait_ge(s["ot"], w + 1)
                    dve.reciprocal(RC[:, :, :, :], Ot[:, :, :, HD:HD + 1]).then_inc(s["rc"], 1)
                    dve.wait_ge(s["rc"], w + 1)
                    if k == 3 and not early(b, k, NG):
                        dve.wait_ge(s["at"], b * TT)
                    dve.tensor_tensor(AO[:, :, g * GH * HD:(g + 1) * GH * HD].rearrange("p i (h d) -> p i h d", d=HD), Ot[:, :, :, 0:HD],
                                      RC[:, :, :, :].broadcast_to([P, TT, GH, HD]), ALU.mult).then_inc(s["nrm"], 1)

                def post(b, n):
                    dve.wait_ge(s["ap"], b * TT + n + 1)
                    if n == 0:
                        dve.wait_ge(s["xb"], b + 1)
                    y = XB[:, n, :]
                    dve.tensor_tensor(y, RIGHT, y, ALU.add).then_inc(s["res"], 1)
                    dve.wait_ge(s["res"], b * TT + n + 1)
                    link(dve.bn_stats(ST6[:, n, :], y))
                    dve.bn_aggr(MV[:, n, :], ST6[:, n, :]).then_inc(s["var"], 1)

                def normal_row(b, n):
                    dve.wait_ge(s["rs"], b * TT + n + 1)
                    dve.tensor_scalar(X1[:, n, :], XB[:, n, :], MV[:, n, 0:1], RS[:, n, :], ALU.subtract, ALU.mult).then_inc(s["x1"], 1)

                def top2(b):
                    dve.wait_ge(s["lgp"], b + 1)
                    dve.tensor_copy(LG[:, :, :], RIGHT[:, 0:TT * NX].rearrange("p (n e) -> p n e", e=NX)).then_inc(s["lg"], 1)
                    settle(dve, s["lg"], b + 1)
                    for n in range(TT):
                        last = dve.max(MVX[:, n, :], LG[:, n, :])
                    link(last)
                    for n in range(TT):
                        last = dve.max_index(MIX[:, n, :], MVX[:, n, :], LG[:, n, :])
                    link(last)
                    dve.tensor_tensor(DL[:, :], MVX[:, :, 1], MVX[:, :, 0], ALU.subtract).then_inc(s["dl"], 1)
                    link(dve.tensor_copy(MIF[:, :, :], MIX[:, :, :]))
                    for k in range(TOPK):
                        last = dve.tensor_tensor(OH[k][:, :, :], iota8.unsqueeze(1).broadcast_to([P, TT, NX]),
                                                 MIF[:, :, k:k + 1].broadcast_to([P, TT, NX]), ALU.is_equal)
                    link(last)
                    dve.tensor_tensor(MC[:, :, :], OH[0][:, :, :], OH[1][:, :, :], ALU.add).then_inc(s["mc"], 1)

                def weights(b):
                    dve.wait_ge(s["ex"], b + 1)
                    link(dve.tensor_scalar(SM[:, :], EX[:, :], 1.0, None, ALU.add))
                    link(dve.reciprocal(WB4[:, :, 0], SM[:, :]))
                    link(dve.tensor_tensor(WB4[:, :, 1], WB4[:, :, 0], EX[:, :], ALU.mult))
                    link(dve.tensor_copy(WT[:, bass.ds(b * TT, TT), :], WB4[:, :, :]))

                def slots(b):
                    dve.wait_ge(s["rkp"], b + 1)
                    dve.tensor_tensor(RK[:, :, :], RIGHT[:, 0:TT * NX].rearrange("p (n e) -> p n e", e=NX),
                                      ebase8.unsqueeze(1).broadcast_to([P, TT, NX]), ALU.add).then_inc(s["rk"], 1)
                    dve.wait_ge(s["rk"], b + 1)
                    for k in range(TOPK):
                        last = dve.tensor_tensor(RKO[k][:, :, :], RK[:, :, :], OH[k][:, :, :], ALU.mult)
                    link(last)
                    settle(dve, s_sc, b * (16 * TT * TOPK) + 16)
                    for k in range(TOPK):
                        last = dve.tensor_reduce(SLF[:, :, k], RKO[k][:, :, :], AX.X, ALU.add)
                    link(last)
                    dve.tensor_copy(SLI[:, :, :], SLF[:, :, :]).then_inc(s["slots"], 1)
                    link(dve.tensor_copy(SLR[:, bass.ds(b * TT * TOPK, TT * TOPK)], SLF[:, :, :].rearrange("p n k -> p (n k)")))
                    link(dve.tensor_reduce(MSUM[:, :], MC[:, :, :].rearrange("p n e -> p e n"), AX.X, ALU.add))
                    dve.tensor_tensor(MRUN[:, :], MRUN[:, :], MSUM[:, :], ALU.add).then_inc(s["mrun"], 1)
                    dve.wait_ge(s["mrun"], b + 2)

                def step(b, k, tails):
                    for n in range(NSG):
                        reduces(b, k, n)
                        if n == OT_AT + 1 and not early(b, k, 3):
                            normalise(b, k)
                        if tails and (k, n) in POST_AT:
                            post(b - 1, POST_AT[k, n])
                        if tails and (k, n) in NORM_AT:
                            normal_row(b - 1, NORM_AT[k, n])
                        if tails and (k, n) == TOP2_AT:
                            top2(b - 1)
                    if tails and k == 3:
                        slots(b - 1)
                    maxima(b, k)
                    if tails and k == 3:
                        weights(b - 1)

                for k in range(NG):
                    step(0, k, False)
                with dve.Fori(1, B) as b:
                    t.enter(b - 1, TT + 4 + 4 + 4)
                    for k in range(NG):
                        step(b, k, True)
                    t.leave(B - 1)
                for k in range(3):
                    normalise(B, k)
                for n in range(TT):
                    post(B - 1, n)
                    if n:
                        normal_row(B - 1, n - 1)
                normal_row(B - 1, TT - 1)
                top2(B - 1)
                slots(B - 1)
                weights(B - 1)
                dve.wait_ge(s["cnt"], 1)
                link(dve.tensor_copy(NF[:, :], RIGHT[:, 0:NX]))
                link(dve.tensor_tensor(GE[:, :, :], NF[:, :].unsqueeze(2).broadcast_to([P, NX, 16]),
                                       thr16.unsqueeze(1).broadcast_to([P, NX, 16]), ALU.is_gt))
                link(dve.tensor_reduce(NT[:, :], GE[:, :, :], AX.X, ALU.add))
                link(dve.tensor_tensor(G8[:, :, :], tri8.rearrange("p (a b) -> p a b", a=NX),
                                       NT[:, :].unsqueeze(1).broadcast_to([P, NX, NX]), ALU.mult))
                link(dve.tensor_reduce(CT[:, :], G8[:, :, :], AX.X, ALU.add))
                link(dve.tensor_tensor(GJ[:, :, :], CT[0:1, :].unsqueeze(1).broadcast_to([1, NTAB, NX]),
                                       jidx[0:1, :].unsqueeze(2).broadcast_to([1, NTAB, NX]), ALU.is_le))
                link(dve.tensor_reduce(EJ[:, :], GJ[:, :, :], AX.X, ALU.add))
                link(dve.tensor_tensor(GP[:, :, :], GJ[:, :, :], NT[0:1, :].unsqueeze(1).broadcast_to([1, NTAB, NX]), ALU.mult))
                link(dve.tensor_reduce(PJ[:, :], GP[:, :, :], AX.X, ALU.add))
                link(dve.tensor_tensor(PJ[:, :], jidx[0:1, :], PJ[:, :], ALU.subtract))
                link(dve.tensor_scalar(PJ[:, :], PJ[:, :], float(P), None, ALU.mult))
                link(dve.scalar_tensor_tensor(RJ[:, :], EJ[:, :], float(REGION), PJ[:, :], ALU.mult, ALU.add))
                link(dve.tensor_copy(TAB[:, 0, :], RJ[:, :]))
                link(dve.tensor_scalar(TAB[:, 1, :], EJ[:, :], float(NX - 1), None, ALU.min))
                link(dve.tensor_scalar(SH[:, :], NT[:, 0:NX - 1], float(P), float(REGION), ALU.mult, ALU.subtract))
                wide = [P, NTT * TOPK, NX - 1]
                link(dve.tensor_tensor(GR[:, :, :], SLR[:, :].unsqueeze(2).broadcast_to(wide), ebase8[:, 1:NX].unsqueeze(1).broadcast_to(wide), ALU.is_ge))
                link(dve.tensor_tensor(GR2[:, :, :], GR[:, :, :], SH[:, :].unsqueeze(1).broadcast_to(wide), ALU.mult))
                link(dve.tensor_reduce(GR[:, :, 0], GR2[:, :, :], AX.X, ALU.add))
                link(dve.tensor_tensor(ROW[:, :], SLR[:, :], GR[:, :, 0], ALU.add))

            @block.tensor
            def _(pe):
                mm = nc.tensor.matmul

                def S(b, k, n):
                    u, p = b * NG + k, k
                    if n == 0:
                        pe.wait_ge(s_kq[k], (b + 1) * (16 * 2 * len(QPART)))
                    after(early(b, k, 1) and n < 2, (pe, s["Sf"], u * NSG + n - 1))
                    dst = Sb[n % 2]

                    def tile_(h, i, at):
                        w = (i + 1) * P
                        mm(dst[:, at:at + w], Q[p][0:SK, h, i * P:(i + 1) * P], K[p][0:SK, h, 0:w], start=True, stop=False)
                        return mm(dst[:, at + w - P:at + w], identb, maskS, start=False, stop=True)

                    if n < 4:
                        last = tile_(n, 3, 0)
                    elif n < 8:
                        tile_(n - 4, 2, 0)
                        last = tile_(n - 4, 0, 3 * P)
                    else:
                        tile_(2 * (n - 8), 1, 0)
                        last = tile_(2 * (n - 8) + 1, 1, 2 * P)
                    last.then_inc(s["S"], 1)

                def where(h, j):
                    if j == 2:
                        return 4, h // 2, 2 * P * (h % 2)
                    return (0 if j == 0 else 2) + h // 2, h % 2, (0, 0, 0, 3 * P)[j]

                def ST(b, k, n):
                    v, g = b * NG + k - 2, (k - 2) % NG
                    if n == 0:
                        pe.wait_ge(s["qm"], v + 1)
                    after(early(b, k, 3) and n < 2, (pe, s["exp"], v * NTG + n - 1))
                    for h in range(GH):
                        for j in range(TT):
                            gr, bk, at = where(h, j)
                            if gr != n:
                                continue
                            dst = STb[slot_of(k, n)][:, bk, :]
                            mm(dst[:, at:at + T - j * P], K[g][0:SKM, h, j * P:(j + 1) * P], Q[g][0:SKM, h, j * P:T], start=True, stop=False)
                            last = mm(dst[:, at:at + P], identb, maskT, start=False, stop=True)
                    last.then_inc(s["ST"], 1)

                def PV(b, k, n, lag=2):
                    v, p = b * NG + k - lag, (k - lag) % 2
                    pe.wait_ge(s["exp"], v * NTG + (2, 4, 5)[n])
                    if n == 0:
                        pe.wait_ge(s["va"], v + 1)
                        after(early(b, k, lag + 1), (pe, s["nrm"], v))
                    for j in ((0,), (1, 3), (2,))[n]:
                        for h in range(GH):
                            gr, bk, at = where(h, j)
                            last = mm(Ob[32 * h:32 * h + 32, j * P:T], VA[p][:, j, h, :], PT[gr][:, bk * T + at:bk * T + at + T - j * P],
                                      start=(j == 0), stop=(j == 2), tile_position=(0, 32 * h))
                    last.then_inc(s["pv"], 1)

                def outputs_T(b, k):
                    pe.wait_ge(s["ocp"], b * NG + k - 2)
                    for i in range(TT):
                        last = nc.tensor.transpose(Ob[:, i * P:(i + 1) * P], O[:, i * P:(i + 1) * P], ident)
                    last.then_inc(s["ot"], 1)

                def maxT(b, k, last_reader):
                    u, p = b * NG + k, (k - 1) % 2
                    if last_reader:
                        pe.wait_ge(*last_reader)
                    pe.wait_ge(s["np"], u)
                    for i in range(TT):
                        last = nc.tensor.transpose(miscb[SK:SKM, i * P:(i + 1) * P], NP[p][:, i, :], identb, tile_position=(0, SK))
                    last.then_inc(s["mt"], 1)

                def ao_T(b, n, last_reader):
                    pe.wait_ge(*last_reader)
                    if n == 0:
                        pe.wait_ge(s["nrm"], b * NG + NG)
                    for k in range(KC):
                        last = nc.tensor.transpose(LEFT[:, k * P:(k + 1) * P], AO[:, n, k * P:(k + 1) * P], ident)
                    last.then_inc(s["at"], 1)

                def out_proj(b, n, last_reader):
                    if last_reader:
                        pe.wait_ge(*last_reader)
                    pe.wait_ge(s["atc"], b * TT + n + 1)
                    for k in range(KC):
                        last = mm(RIGHT, XT1[:, n, k, :], WP[:, k, :], start=(k == 0), stop=(k == KC - 1))
                    last.then_inc(s["ap"], 1)

                def x1_T(b, n, last_reader):
                    pe.wait_ge(*last_reader)
                    pe.wait_ge(s["x1"], b * TT + n + 1)
                    for k in range(KC):
                        last = nc.tensor.transpose(LEFT[:, k * P:(k + 1) * P], X1[:, n, k * P:(k + 1) * P], ident)
                    last.then_inc(s["tp"], 1)

                def logits(b, last_reader):
                    pe.wait_ge(*last_reader)
                    pe.wait_ge(s["xt"], b * TT + TT)
                    for n in range(TT):
                        for k in range(KC):
                            last = mm(RIGHT[:, n * NX:(n + 1) * NX], XT1[:, n, k, :], RW[:, k, :], start=(k == 0), stop=(k == KC - 1))
                    last.then_inc(s["lgp"], 1)

                def ranks(b, last_reader):
                    pe.wait_ge(*last_reader)
                    pe.wait_ge(s["mc"], b + 1)
                    pe.wait_ge(s["mrun"], b + 1)
                    for n in range(TT):
                        dst = RIGHT[:, n * NX:(n + 1) * NX]
                        mm(dst, tri, MC[:, n, :], start=True, stop=False)
                        for m in range(n):
                            mm(dst, onesb, MC[:, m, :], start=False, stop=False)
                        last = mm(dst, onesb, MRUN[:, :], start=False, stop=True)
                    last.then_inc(s["rkp"], 1)

                def step(b, k, tails):
                    u, r = b * NG + k, b - 1
                    reader = None if k == 0 or early(b, k, 2) else (s["atc"], r * TT + TT - 1) if tails and k == 3 else (s["qm"], u - 1)
                    for n in range(NSG):
                        S(b, k, n)
                        if n in ST_AT and not early(b, k, 2):
                            ST(b, k, ST_AT[n])
                        if n in PV_AT and not early(b, k, 3 if n == 1 else 2):
                            PV(b, k, PV_AT[n], 3 if n == 1 else 2)
                        if n == OT_AT and not early(b, k, 3):
                            outputs_T(b, k)
                        if tails and (k, n) in AT_AT:
                            ao_T(r, AT_AT[k, n], reader)
                            reader = (s["atc"], r * TT + AT_AT[k, n] + 1)
                        if tails and (k, n) in OUT_AT:
                            out_proj(r, OUT_AT[k, n], reader)
                            reader = (s["res"], r * TT + OUT_AT[k, n] + 1)
                        if tails and (k, n) in XT_AT:
                            x1_T(r, XT_AT[k, n], reader)
                            reader = (s["xt"], r * TT + XT_AT[k, n] + 1)
                        if n == MAXT_AT[k] and not early(b, k, 1):
                            maxT(b, k, reader)
                            reader = (s["qm"], u)
                        if tails and (k, n) == LOGITS_AT:
                            logits(r, reader)
                        if tails and (k, n) == RANKS_AT:
                            ranks(r, (s["lg"], b))

                for k in range(NG):
                    step(0, k, False)
                with pe.Fori(1, B) as b:
                    for k in range(NG):
                        step(b, k, True)
                ST(B, 0, 0)
                PV(B, 0, 2, 3)
                ST(B, 0, 1)
                maxT(B, 0, (s["qm"], NU - 1))
                outputs_T(B, 0)
                for n in range(2, NTG):
                    ST(B, 0, n)
                PV(B, 0, 0)
                PV(B, 0, 1)
                ST(B, 1, 0)
                PV(B, 1, 2, 3)
                ST(B, 1, 1)
                outputs_T(B, 1)
                for n in range(2, NTG):
                    ST(B, 1, n)
                PV(B, 1, 0)
                PV(B, 1, 1)
                PV(B, 2, 2, 3)
                outputs_T(B, 2)
                r = B - 1
                reader = (s["qm"], NU)
                for n in range(TT):
                    ao_T(r, n, reader)
                    out_proj(r, n, (s["atc"], r * TT + n + 1))
                    reader = (s["res"], r * TT + n + 1)
                for n in range(TT):
                    x1_T(r, n, reader)
                    reader = (s["xt"], r * TT + n + 1)
                logits(r, reader)
                ranks(B - 1, (s["lg"], B))
                pe.wait_ge(s["rk"], B)
                pe.wait_ge(s["mrun"], B + 1)
                mm(RIGHT[:, 0:NX], onesb, MRUN[:, :], start=True, stop=True).then_inc(s["cnt"], 1)

        f = {n: sem("c_" + n) for n in ("xt", "xgt", "g", "u", "sil", "h", "th", "ht", "yp", "ys")}
        s_idx, s_g, s_yw = ([sem(f"s_{n}{q}") for q in range(TRIO)] for n in ("idx", "xg", "yw"))
        NTRIO = NTILES // TRIO
        G, U, XP, HP, YP = bank[0], bank[1], bank[2], bank[3], bank[4]

        with nc.Block() as block:
            @block.sync
            def _(sp):
                def first_slot(j):
                    return sp.value_load(TAB[0:1, 0, bass.ds(j, 1)], min_val=0, max_val=NSLOT - P)

                def fetch_tokens(i, q):
                    at = first_slot(i * TRIO + q)
                    sp.dma_start(IDX[q][:, :], tok_dram[bass.ds(at, P), :]).then_inc(s_idx[q], 16)

                for q in range(TRIO):
                    fetch_tokens(0, q)
                with sp.Fori(0, NTRIO) as i:
                    for q in range(TRIO):
                        sp.wait_ge(s_g[q], i * 16 + 16)
                        fetch_tokens(i + 1, q)
                        sp.wait_ge(f["ys"], i * TRIO + q + 1)
                        sp.dma_start(y_dram[bass.ds((i * TRIO + q) * P, P), :], YS[q]).then_inc(s_yw[q], 16)
                for q in range(TRIO):
                    sp.wait_ge(s_yw[q], 16 * NTRIO)

            @block.gpsimd
            def _(pool):
                def gather(i, q):
                    settle(pool, s_idx[q], i * 16 + 16)
                    pool.indirect_dma_start(XG[q], None, x1_dram, bass.IndirectOffsetOnAxis(ap=IDX[q][:, :], axis=0)).then_inc(s_g[q], 16)

                for q in range(TRIO):
                    gather(0, q)
                with pool.Fori(0, NTRIO) as i:
                    for q in range(TRIO):
                        settle(pool, f["xt"], i * TRIO + q + 1)
                        gather(i + 1, q)
                for q in range(TRIO):
                    settle(pool, s_g[q], 16 * (NTRIO + 1))

            @block.scalar
            def _(act):
                def columns(j):
                    act.wait_ge(f["xt"], j + 1)
                    act.activation(XGT.rearrange("p k t -> p (k t)"), XP[:, 0:E], ACT.Copy).then_inc(f["xgt"], 1)

                def silu(j):
                    act.wait_ge(f["g"], j + 1)
                    act.activation(SIL, G, ACT.Silu).then_inc(f["sil"], 1)

                def result(i, q, j):
                    act.wait_ge(f["yp"], j + 1)
                    after(isinstance(i, int) and i == 0, (act, s_yw[q], i * 16))
                    act.activation(YS[q], YP[:, 0:E], ACT.Copy).then_inc(f["ys"], 1)

                def tile_(i, q):
                    j = i * TRIO + q
                    silu(j)
                    if q:
                        result(i, q - 1, j - 1)
                    elif not (isinstance(i, int) and i == 0):
                        result(i - 1, TRIO - 1, j - 1)
                    columns(j + 1)

                columns(0)
                for i in range(2):
                    for q in range(TRIO):
                        tile_(i, q)
                with act.Fori(2, NTRIO) as i:
                    for q in range(TRIO):
                        tile_(i, q)
                result(NTRIO - 1, TRIO - 1, NTILES - 1)

            @block.vector
            def _(dve):
                def tile_(j):
                    dve.wait_ge(f["sil"], j + 1)
                    dve.wait_ge(f["u"], j + 1)
                    after(isinstance(j, int) and j == 0, (dve, f["th"], j))
                    dve.tensor_tensor(HH, U, SIL, ALU.mult).then_inc(f["h"], 1)
                    dve.wait_ge(f["th"], j + 1)
                    after(isinstance(j, int) and j == 0, (dve, f["yp"], j))
                    dve.tensor_copy(HT.rearrange("p k t -> p (k t)"), HP).then_inc(f["ht"], 1)

                tile_(0)
                with dve.Fori(1, NTILES) as j:
                    tile_(j)

            @block.tensor
            def _(pe):
                mm = nc.tensor.matmul

                def expert(j):
                    return pe.value_load(TAB[0:1, 1, bass.ds(j, 1)], min_val=0, max_val=NX - 1)

                def rows_T(i, q, j):
                    pe.wait_ge(s_g[q], i * 16 + 16)
                    after(isinstance(j, int) and j == 0, (pe, f["xgt"], j))
                    for k in range(KC):
                        last = nc.tensor.transpose(XP[:, k * P:(k + 1) * P], XG[q][:, k * P:(k + 1) * P], ident)
                    last.then_inc(f["xt"], 1)

                def up(j, e):
                    first = isinstance(j, int) and j == 0
                    pe.wait_ge(f["xgt"], j + 1)
                    for dst, n, done, used in ((G, 0, f["g"], f["sil"]), (U, 1, f["u"], f["h"])):
                        after(first, (pe, used, j))
                        for k in range(KC):
                            at = (e + k * NX) * (2 * FF) + n * FF
                            last = mm(dst, XGT[:, k, :], W1[:, bass.ds(at, FF)], start=(k == 0), stop=(k == KC - 1))
                        last.then_inc(done, 1)

                def hidden_T(j):
                    pe.wait_ge(f["h"], j + 1)
                    after(isinstance(j, int) and j == 0, (pe, f["ht"], j))
                    for k in range(FF // P):
                        last = nc.tensor.transpose(HP[:, k * P:(k + 1) * P], HH[:, k * P:(k + 1) * P], ident)
                    last.then_inc(f["th"], 1)

                def down(j, e):
                    pe.wait_ge(f["ht"], j + 1)
                    after(isinstance(j, int) and j == 0, (pe, f["ys"], j))
                    for k in range(FF // P):
                        last = mm(YP[:, 0:E], HT[:, k, :], W2[:, bass.ds((e + k * NX) * E, E)], start=(k == 0), stop=(k == FF // P - 1))
                    last.then_inc(f["yp"], 1)

                def trio(i):
                    e_before = None
                    for q in range(TRIO):
                        j = i * TRIO + q
                        e = expert(j)
                        up(j, e)
                        if q:
                            down(j - 1, e_before)
                        elif not isinstance(i, int):
                            down(j - 1, expert(j - 1))
                        if q < TRIO - 1:
                            rows_T(i, q + 1, j + 1)
                        else:
                            rows_T(i + 1, 0, j + 1)
                        hidden_T(j)
                        e_before = e

                rows_T(0, 0, 0)
                trio(0)
                with pe.Fori(1, NTRIO) as i:
                    trio(i)
                down(NTILES - 1, expert(NTILES - 1))

        d = {n: sem("d_" + n) for n in ("idx", "dve", "sum", "out", "pool", "var", "rs")}
        s_yg, s_xl, s_st = [sem(f"s_yg{n}") for n in range(TT)], sem("s_xl"), [sem(f"s_st{n}") for n in range(TT)]
        YG = [[PT[n][:, k * E:(k + 1) * E] for k in range(TOPK)] for n in range(TT)]
        OUT = [PT[n][:, 2 * E:3 * E] for n in range(TT)]
        XR = [XB, X1]

        with nc.Block() as block:
            @block.sync
            def _(sp):
                def load(b, dst):
                    after(early(b, 0, 1), (sp, d["out"], b * TT))
                    sp.dma_start(dst[:, :, :], x1_dram[bass.ds(b * T, T), :].rearrange("(n p) f -> p n f", p=P)).then_inc(s_xl, 16)

                load(0, X1)
                def store(b):
                    for n in range(TT):
                        sp.wait_ge(d["out"], b * TT + n + 1)
                        sp.dma_start(out[bass.ds(b * T + n * P, P), :], OUT[n]).then_inc(s_st[n], 16)

                store(0)
                with sp.Fori(1, B) as b:
                    load(b, X1)
                    store(b)
                for n in range(TT):
                    sp.wait_ge(s_st[n], 16 * B)

            @block.gpsimd
            def _(pool):
                def gather(b, first):
                    if not first:
                        for n in range(TT):
                            settle(pool, s_yg[n], b * 32)
                    pool.tensor_copy(IDG[:, :, :].rearrange("p n k -> p (n k)"), ROW[:, bass.ds(b * TT * TOPK, TT * TOPK)]).then_inc(d["idx"], 1)
                    settle(pool, d["idx"], b + 1)
                    for n in range(TT):
                        if not first:
                            settle(pool, d["sum"], (b - 1) * TT + n + 1)
                        for k in range(TOPK):
                            pool.indirect_dma_start(YG[n][k], None, y_dram, bass.IndirectOffsetOnAxis(ap=IDG[:, n, k:k + 1], axis=0)).then_inc(s_yg[n], 16)

                t = Tally()

                def inverse_std(b):
                    for n in range(TT):
                        settle(pool, d["var"], b * TT + n + 1)
                        pool.tensor_scalar(VE[:, n, :], MV[:, n, 1:2], EPS, None, ALU.add).then_inc(d["pool"], 1)
                        settle(pool, d["pool"], t.step())
                        pool.tensor_tensor(RS[:, n, :], VE[:, n, :], MHALF[:, :], ALU.pow).then_inc(d["rs"], 1)

                gather(0, True)
                inverse_std(0)
                with pool.Fori(1, B) as b:
                    t.enter(b - 1, TT)
                    gather(b, False)
                    inverse_std(b)
                    t.leave(B - 1)

            @block.vector
            def _(dve):
                t = Tally()

                def link(ins):
                    ins.then_inc(d["dve"], 1)
                    settle(dve, d["dve"], t.step())

                def tile_(b, n, first):
                    dve.wait_ge(s_xl, b * 16 + 16)
                    dve.wait_ge(s_yg[n], b * 32 + 32)
                    w = WT[:, bass.ds(b * TT + n, 1), :].rearrange("p o k -> p (o k)")
                    y = X1[:, n, :]
                    link(dve.scalar_tensor_tensor(y, YG[n][0], w[:, 0:1], y, ALU.mult, ALU.add))
                    dve.scalar_tensor_tensor(y, YG[n][1], w[:, 1:2], y, ALU.mult, ALU.add).then_inc(d["sum"], 1)
                    dve.wait_ge(d["sum"], b * TT + n + 1)
                    link(dve.bn_stats(ST6[:, n, :], y))
                    dve.bn_aggr(MV[:, n, :], ST6[:, n, :]).then_inc(d["var"], 1)

                def normal_row(b, n, first):
                    y = X1[:, n, :]
                    dve.wait_ge(d["rs"], b * TT + n + 1)
                    if not first:
                        dve.wait_ge(s_st[n], b * 16)
                    dve.tensor_scalar(OUT[n], y, MV[:, n, 0:1], RS[:, n, :], ALU.subtract, ALU.mult).then_inc(d["out"], 1)

                for n in range(TT):
                    tile_(0, n, True)
                for n in range(TT):
                    normal_row(0, n, True)
                with dve.Fori(1, B) as b:
                    t.enter(b - 1, 2 * TT)
                    for n in range(TT):
                        tile_(b, n, False)
                    for n in range(TT):
                        normal_row(b, n, False)
                    t.leave(B - 1)


def constants():
    f32 = np.float32
    cf = np.zeros((P, 224 + NTAB), f32)
    cf[:, 0:P] = np.eye(P)
    cf[:, 128:136] = np.arange(NX)
    cf[:, 136:144] = np.arange(NX) * REGION
    cf[:, 144:160] = np.arange(16) * P
    cf[:, 160:224] = np.tril(np.ones((NX, NX))).reshape(-1)
    cf[:, 224:224 + NTAB] = np.arange(NTAB)
    bf = np.dtype("bfloat16")
    row, col = np.arange(P)[:, None], np.arange(P)[None, :]
    low = f32(-1e30)
    cb = np.concatenate([row == col, (col > row) * low, (row > col) * low, row < col, np.ones((P, P))], 1).astype(bf)
    kones = np.zeros((PARTS * GH, GH, T), bf)
    for r in range(PARTS):
        for h in range(GH):
            kones[r * GH + h, h, :] = 1
    freqs = f32(10000.0) ** (-(np.arange(0, HD, 2, dtype=f32) / f32(HD)))
    angle = np.outer(np.arange(H, dtype=f32), freqs).astype(f32).reshape(1, -1)
    cos_sin = np.concatenate([np.cos(angle), np.sin(angle)], 0).astype(f32)
    tokid = (np.arange(NTT)[None, :] * P + np.arange(P)[:, None]).astype(np.int32)
    return cf, cb, kones, cos_sin, tokid


def kernel(**inputs):
    import concourse.bacc as _bacc
    from concourse.bass_utils import run_bass_kernel_spmd as _run

    a = {k: np.asarray(v) for k, v in inputs.items()}
    x = a["L0_attn_x"].reshape(NTOK, E)
    cf, cb, kones, cos_sin, tokid = constants()
    arrays = {
        "x": x, "xT": x.T, "w_attn": a["L0_attn_w_attn"], "b_attn": a["L0_attn_b_attn"], "w_proj": a["L0_attn_w_proj"].reshape(KC, P, E),
        "b_proj": a["L0_attn_b_proj"], "router_wT": a["L0_ffn_router_w"].T,
        "w1T": a["L0_ffn_ws"].transpose(2, 0, 1).reshape(KC, P, NX, 2 * FF).transpose(1, 0, 2, 3).reshape(P, -1),
        "w2T": a["L0_ffn_w2s"].transpose(2, 0, 1).reshape(FF // P, P, NX, E).transpose(1, 0, 2, 3).reshape(P, -1),
        "cos_sin": cos_sin, "cf": cf, "cb": cb, "kones": kones, "tokid": tokid,
    }
    arrays = {k: np.ascontiguousarray(v) for k, v in arrays.items()}
    nc = _bacc.Bacc("TRN2", target_bir_lowering=False, num_devices=1)
    args = {k: nc.dram_tensor(k, v.shape, mybir.dt.from_np(v.dtype), kind="ExternalInput").ap() for k, v in arrays.items()}
    out = nc.dram_tensor("out", (NTOK, E), F32, kind="ExternalOutput").ap()
    block_kernel(nc, out=out, **args)
    r = _run(nc, [arrays], core_ids=[0])
    return r.results[0]["out"].reshape(B, T, E)
```

```python
import concourse.bass as bass
from concourse import mybir
from contextlib import ExitStack
import numpy as np

F32 = mybir.dt.float32
BF16 = mybir.dt.bfloat16
F16 = mybir.dt.float16
I32 = mybir.dt.int32
U32 = mybir.dt.uint32
ALU = mybir.AluOpType
ACT = mybir.ActivationFunctionType
AX = mybir.AxisListType

P = 128
B, T, E = 4, 512, 256
H, HD = 16, 16
NTOK = B * T
NTT = NTOK // P
TT = T // P
KC = E // P
NG = 4
GH = H // NG
NU = B * NG
PARTS = 3
QPART = [0, 0, 0, 1, 1, 2]
KPART = [0, 1, 2, 0, 1, 0]
SK = HD * len(QPART)
SKM = SK + PARTS * GH
NX, FF, TOPK = 8, 512, 2
REGION = NTOK
NTILES = NTOK * TOPK // P + NX - 1
TRIO = 3
NTAB = NTILES + TRIO
NSLOT = NX * REGION + NTAB * P
EPS = 1e-5
LOW = -3e38
XSCALE = 2.0 ** 11
WSCALE = 2.0 ** 15
UNIT = FF
NUNIT = KC * NX * 2
SPARE = 2 * UNIT
NSG, NTG = 10, 5


class Tally:

    def __init__(self):
        self.base, self.n = 0, 0

    def step(self):
        self.n += 1
        return self.base + self.n

    def enter(self, trip, per):
        self.start, self.per, self.n = self.base + self.n, per, 0
        self.base = trip * per + self.start

    def leave(self, trips):
        assert self.n == self.per, (self.n, self.per)
        self.base, self.n = self.start + trips * self.per, 0


def block_kernel(nc, x, xT, w_attn, b_attn, w_proj, b_proj, router_wT, w1T, w2T, cos_sin, cf, cb, kones, tokid, unused, out):
    ctx = ExitStack()
    with ctx:
        def sb(name, shape, dt=F32):
            return ctx.enter_context(nc.sbuf_tensor(name, shape, dt))

        def sem(name):
            return ctx.enter_context(nc.semaphore(name))

        def dram(name, shape, dt):
            return nc.dram_tensor(name, shape, dt, kind="Internal").ap()

        qk_dram = dram("qk_parts", (2, PARTS, E, NTOK), BF16)
        x1_dram = dram("x1_rows", (NTOK + P, 2 * E), F16)
        acc_dram = dram("sum_rows", (NTOK + P, E), F32)
        tok_dram = dram("slot_token", (NSLOT, 2), I32)

        W1 = sb("W1", [P, SPARE + NUNIT * UNIT])
        w1h = W1[:, :].bitcast(F16)
        W2 = sb("W2", [P, 4 * NX * E])
        CF = sb("CF", [P, cf.shape[1]])
        ident = CF[:, 0:P]
        iota8, ebase8 = CF[:, 128:136], CF[:, 136:144]
        thr16, tri8, jidx = CF[:, 144:160], CF[:, 160:224], CF[:, 224:224 + NTAB]
        CB = sb("CB", [P, 8 * P], BF16)
        identb, maskT, tri, onesb = (CB[:, n * P:(n + 1) * P] for n in range(4))
        maskS = CB[:, 4 * P:8 * P]
        WP = sb("WP", [P, 2, E])
        RW = sb("RW", [P, KC, NX])
        BP = sb("BP", [P, E])
        VR = sb("VR", [P, NTT, E])
        X1 = sb("X1", [P, TT, E])
        X1S = sb("X1S", [P, TT, 2, E], F16)
        IDH = sb("IDH", [P, P], F16)
        ONESF = sb("ONESF", [P, P])
        SQ = sb("SQ", [P, KC * NX])
        F2 = [sb(f"F2{n}", [P, 1]) for n in range(2)]
        ROOT = [sb(f"ROOT{n}", [P, 1]) for n in range(2)]
        HALF = sb("HALF", [P, 1])
        SW = sb("SW", [P, 1])
        CW = sb("CW", [P, 1])
        TOK = sb("TOK", [P, NTT], I32)
        TAB = sb("TAB", [1, 2, NTAB], I32)
        K = [sb(f"K{g}", [P, GH, T], BF16) for g in range(NG)]
        Q = [sb(f"Q{g}", [P, GH, T], BF16) for g in range(NG)]
        VA = [sb(f"VA{p}", [P, TT, GH, 2 * HD]) for p in range(2)]
        O = sb("O", [P, T])
        PT = [sb(f"PT{n}", [P, 2 * T]) for n in range(NTG)]
        RC = sb("RC", [P, TT, GH, 1])
        AO = sb("AO", [P, TT, E])
        MX = [sb(f"MX{p}", [P, GH, TT]) for p in range(2)]
        NM = sb("NM", [P, 2, TT, GH])
        NP = [sb(f"NP{p}", [P, TT, PARTS * GH], BF16) for p in range(2)]
        XB = sb("XB", [P, TT, E])
        ST6 = sb("ST6", [P, TT, 6])
        MV = sb("MV", [P, TT, 2])
        VE = sb("VE", [P, TT, 1])
        RS = sb("RS", [P, TT, 1])
        MHALF = sb("MHALF", [P, 1])
        XT1 = sb("XT1", [P, TT, KC, P])
        LG = sb("LG", [P, TT, NX])
        MVX = sb("MVX", [P, TT, 8])
        MIX = sb("MIX", [P, TT, 8], U32)
        MIF = sb("MIF", [P, TT, 8])
        OH = [sb(f"OH{k}", [P, TT, NX]) for k in range(TOPK)]
        MC = sb("MC", [P, TT, NX], BF16)
        MRUN = sb("MRUN", [P, NX], BF16)
        MSUM = sb("MSUM", [P, NX])
        DL = sb("DL", [P, TT])
        EX = sb("EX", [P, TT])
        SM = sb("SM", [P, TT])
        RK = sb("RK", [P, TT, NX])
        RKO = [sb(f"RKO{k}", [P, TT, NX]) for k in range(TOPK)]
        SLF = sb("SLF", [P, TT, TOPK])
        SLI = sb("SLI", [P, TT, TOPK], I32)
        PAIRF = sb("PAIR", [P, TT, TOPK, 2])
        PAIR = PAIRF[:, :, :, :].rearrange("p n k o -> p (n k o)").bitcast(I32).rearrange("p (n k o) -> p n k o", n=TT, k=TOPK)
        WA = W1[:, 0:2304].rearrange("p (k f) -> p k f", k=3)
        WR = W1[:, 2304:3840].rearrange("p (k f) -> p k f", k=3)
        RT = W1[:, 3840:4096].rearrange("p (k f) -> p k f", k=2)
        RTMP = W1[:, 4096:5120].rearrange("p (k f) -> p k f", k=4)
        XTB = [W1[:, 5120 + 1024 * n:6144 + 1024 * n].rearrange("p (k t) -> p k t", k=KC) for n in range(B)]
        QF = [W1[:, 9216 + 512 * n:9728 + 512 * n] for n in range(4)]
        R1 = [W1[:, 11264 + 512 * n:11776 + 512 * n] for n in range(4)]
        PB = [W1[:, 13312 + 768 * n:14080 + 768 * n].bitcast(BF16).rearrange("p (r t) -> p r t", r=3) for n in range(4)]
        BC = sb("BC", [P, 4])
        ONE = sb("ONE", [P, 1])
        EX0 = sb("EX0", [P, 1])
        XG = [PT[0][:, 256 * n:256 * n + 256].bitcast(F16) for n in range(3)]
        XGT = [PT[1][:, 256 * n:256 * n + 256].bitcast(F16).rearrange("p (r k t) -> p r k t", r=2, k=KC) for n in range(3)]
        SIL, HH = PT[2][:, 0:512], PT[2][:, 512:1024]
        HT = PT[3][:, 0:512].rearrange("p (k t) -> p k t", k=4)
        YS = [PT[4][:, 256 * n:256 * n + 256] for n in range(3)]
        IDX = [sb(f"IDX{n}", [P, 2], I32) for n in range(TRIO)]
        IDW = [sb(f"IDW{n}", [P, 2], I32) for n in range(TRIO)]
        NF = sb("NF", [P, NX])
        GE = sb("GE", [P, NX, 16])
        NT = sb("NT", [P, NX])
        CT = sb("CT", [P, NX])
        G8 = sb("G8", [P, NX, NX])
        GJ, GP = (XT1[0:1, :, :, :].rearrange("p n k t -> p (n k t)")[:, n * NTAB * NX:(n + 1) * NTAB * NX].rearrange("p (j e) -> p j e", e=NX) for n in range(2))
        EJ = sb("EJ", [1, NTAB])
        PJ = sb("PJ", [1, NTAB])
        RJ = sb("RJ", [1, NTAB])

        PS = ctx.enter_context(nc.psum_tensor("PS", [P, 8, 512], F32))
        bank = [PS[:, n, :] for n in range(8)]
        Sb = [bank[0], bank[1]]
        STb = [PS[:, 2 + 2 * n:4 + 2 * n, :] for n in range(2)]
        Ob = bank[6]
        MISC = bank[7]
        Ot = MISC.rearrange("p (i h d) -> p i h d", i=TT, h=GH)
        maxb = Ob.bitcast(BF16)

        s_zero, s_wv = sem("s_zero"), sem("s_wv")
        s_const, s_rope, s_x = sem("s_const"), sem("s_rope"), [sem(f"s_x{b}") for b in range(B)]
        s_sync = {n: sem("a_" + n) for n in ("init", "one", "dve", "wr", "bias", "bc", "ps", "vps", "qf", "h", "r", "m", "l", "v", "rb")}
        a = s_sync
        s_pb = [sem(f"s_pb{c}") for c in range(4)]

        names = ("S", "Sf", "np", "pool", "qm", "ST", "exp", "pv", "va", "ocp", "ot", "rc", "nrm",
                 "mt", "at", "atc", "ap", "res", "x1", "xb", "tp", "xt", "lgp", "lg", "mc", "rkp", "rk", "mrun", "dve", "dl", "ex", "slots",
                 "cnt", "var", "rs", "wts", "tab", "xh", "xl", "sq", "sqp", "f2", "root", "sc", "hi", "lo")
        s = {n: sem("b_" + n) for n in names}
        s_kq = [sem(f"s_kq{g}") for g in range(NG)]
        s_w1 = sem("s_w1")
        s_xb, s_x1w, s_w, s_sc = sem("s_xb"), sem("s_x1w"), sem("s_w"), sem("s_sc")

        block = ctx.enter_context(nc.Block())

        V_FIRST, V_AFTER = (0, 1, 2), ((3, 4), (5, 6), (7,), ())

        def rope_views(k):
            pairs = [src[:, k, 0:2 * E].rearrange("p (q f two) -> p two q f", two=2, q=2) for src in (WA, WR)]
            return [[pair[:, n, :, :] for n in range(2)] for pair in pairs] + [[RT[:, n, :].unsqueeze(1).broadcast_to([P, 2, P]) for n in range(2)]]

        @block.sync
        def _(sp):
            def load_x(b):
                sp.dma_start(XTB[b], xT[:, b * T:(b + 1) * T].rearrange("(k p) t -> p k t", p=P)).then_inc(s_x[b], 16)

            sp.dma_start(WA[:, 0:2, 2 * E:3 * E], w_attn[:, 2 * E:3 * E].rearrange("(k p) f -> p k f", p=P)).then_inc(s_wv, 16)
            load_x(0)
            sp.dma_start(RT, cos_sin.partition_broadcast(P)).then_inc(s_rope, 16)
            sp.dma_start(WA[:, 2, :], b_attn.partition_broadcast(P)).then_inc(s_rope, 16)
            sp.dma_start(WA[:, 0:2, 0:2 * E], w_attn[:, 0:2 * E].rearrange("(k p) f -> p k f", p=P)).then_inc(s_rope, 16)
            for b in range(1, B):
                load_x(b)
            sp.wait_ge(a["init"], 1)
            sp.dma_start(x1_dram[NTOK:NTOK + P, :], AO[:, 0, :].bitcast(F16)).then_inc(s_zero, 16)
            sp.dma_start(acc_dram[NTOK:NTOK + P, :], AO[:, 0, :]).then_inc(s_zero, 16)

        @block.gpsimd
        def _(pool):
            pool.dma_start(tok_dram, unused).then_inc(s_sc, 16)
            pool.wait_ge(s_rope, 48)
            tmp = [W2[:, n * E:(n + 1) * E].rearrange("p (q f) -> p q f", q=2) for n in range(4)]
            (even, odd), (reven, rodd), (cos, sin) = rope_views(2)
            pool.tensor_tensor(tmp[0], even, cos, ALU.mult)
            pool.tensor_tensor(tmp[1], odd, sin, ALU.mult)
            pool.tensor_tensor(tmp[2], even, sin, ALU.mult)
            pool.tensor_tensor(tmp[3], odd, cos, ALU.mult).then_inc(a["rb"], 1)
            pool.wait_ge(a["rb"], 1)
            pool.tensor_tensor(reven, tmp[0], tmp[1], ALU.subtract)
            pool.tensor_tensor(rodd, tmp[2], tmp[3], ALU.add).then_inc(a["rb"], 1)
            pool.wait_ge(s_sc, 16)

        @block.scalar
        def _(act):
            act.wait_ge(s_rope, 48)
            act.dma_start(CF[:, :], cf).then_inc(s_const, 16)
            act.dma_start(CB[:, :], cb).then_inc(s_const, 16)
            for g in range(NG):
                act.dma_start(K[g][SK:SKM, :, :], kones).then_inc(s_const, 16)
            act.dma_start(WP[:, :, :], w_proj.rearrange("c p f -> p c f")).then_inc(s_const, 16)
            act.dma_start(RW[:, :, :], router_wT.rearrange("(k p) e -> p k e", p=P)).then_inc(s_const, 16)
            act.dma_start(BP[:, :], b_proj.partition_broadcast(P)).then_inc(s_const, 16)
            act.dma_start(TOK[:, :], tokid).then_inc(s_const, 16)

            def middle_part(b, c):
                act.wait_ge(a["r"], 4 * b + c + 1)
                act.activation(PB[c][:, 1, :], R1[c], ACT.Copy).then_inc(a["m"], 1)

            act.wait_ge(a["bc"], 1)
            for b in range(B):
                for c in range(4):
                    act.wait_ge(a["ps"], 4 * b + c + 1)
                    if b:
                        act.wait_ge(a["l"], 4 * (b - 1) + c + 1)
                    act.activation(QF[c], bank[c], ACT.Identity, bias=BC[:, c:c + 1]).then_inc(a["qf"], 1)
                    act.wait_ge(a["qf"], 4 * b + c + 1)
                    if b:
                        act.wait_ge(s_pb[c], 16 * b)
                    act.activation(PB[c][:, 0, :], QF[c], ACT.Copy).then_inc(a["h"], 1)
                    if c:
                        middle_part(b, c - 1)
                middle_part(b, 3)

        @block.vector
        def _(dve):
            t = Tally()

            def link(ins):
                ins.then_inc(a["dve"], 1)
                dve.wait_ge(a["dve"], t.step())

            dve.memset(AO[:, 0, :], 0.0).then_inc(a["init"], 1)
            dve.memset(ONE[:, :], 1.0).then_inc(a["one"], 1)
            dve.memset(MHALF[:, :], -0.5)
            dve.memset(HALF[:, :], 0.5)
            dve.memset(ONESF[:, :], 1.0)
            dve.memset(SQ[:, :], 0.0).then_inc(s["sq"], 1)
            dve.memset(MRUN[:, :], 0.0).then_inc(s["mrun"], 1)
            for p in range(2):
                dve.memset(VA[p][:, :, :, :], float(E) ** 0.5)
            dve.wait_ge(s_rope, 48)
            for k in range(KC):
                tmp = [RTMP[:, n, :].rearrange("p (q f) -> p q f", q=2) for n in range(4)]
                (even, odd), (reven, rodd), (cos, sin) = rope_views(k)
                if k:
                    dve.wait_ge(a["wr"], k)
                dve.tensor_tensor(tmp[0], even, cos, ALU.mult)
                dve.tensor_tensor(tmp[1], odd, sin, ALU.mult)
                dve.tensor_tensor(tmp[2], even, sin, ALU.mult)
                link(dve.tensor_tensor(tmp[3], odd, cos, ALU.mult))
                dve.tensor_tensor(reven, tmp[0], tmp[1], ALU.subtract)
                dve.tensor_tensor(rodd, tmp[2], tmp[3], ALU.add).then_inc(a["wr"], 1)
            dve.wait_ge(a["bias"], 1)
            dve.tensor_copy(BC[:, :], MISC[:, 0:4]).then_inc(a["bc"], 1)

            def values(v):
                dve.wait_ge(a["vps"], v + 1)
                dve.tensor_tensor(VR[:, 2 * v:2 * v + 2, :], bank[4 + v % 3].rearrange("p (n f) -> p n f", n=2),
                                  WA[:, 2, 2 * E:3 * E].unsqueeze(1).broadcast_to([P, 2, E]), ALU.add).then_inc(a["v"], 1)

            def last_part(b, c):
                dve.wait_ge(a["m"], 4 * b + c + 1)
                dve.tensor_tensor(PB[c][:, 2, :], R1[c], PB[c][:, 1, :], ALU.subtract).then_inc(a["l"], 1)

            for v in V_FIRST:
                values(v)
            for b in range(B):
                for c in range(4):
                    dve.wait_ge(a["h"], 4 * b + c + 1)
                    dve.tensor_tensor(R1[c], QF[c], PB[c][:, 0, :], ALU.subtract).then_inc(a["r"], 1)
                    if c:
                        last_part(b, c - 1)
                last_part(b, 3)
                for v in V_AFTER[b]:
                    values(v)

        @block.tensor
        def _(pe):
            def values(v):
                pe.wait_ge(s_x[v // 2], 16)
                if v >= 3:
                    pe.wait_ge(a["v"], v - 2)
                for n in range(2):
                    t0 = (2 * (v % 2) + n) * P
                    for k in range(KC):
                        last = nc.tensor.matmul(bank[4 + v % 3][:, n * E:(n + 1) * E], XTB[v // 2][:, k, t0:t0 + P],
                                                WA[:, k, 2 * E:3 * E], start=(k == 0), stop=(k == KC - 1))
                last.then_inc(a["vps"], 1)

            pe.wait_ge(s_wv, 16)
            for v in V_FIRST:
                values(v)
            pe.wait_ge(a["wr"], 2)
            pe.wait_ge(a["rb"], 2)
            pe.wait_ge(a["one"], 1)
            for c in range(4):
                last = nc.tensor.matmul(MISC[:, c:c + 1], WR[0:1, 2, c * P:(c + 1) * P], ONE[0:1, :], start=True, stop=True)
            last.then_inc(a["bias"], 1)
            for b in range(B):
                for c in range(4):
                    if b:
                        pe.wait_ge(a["qf"], 4 * (b - 1) + c + 1)
                    for k in range(KC):
                        last = nc.tensor.matmul(bank[c], WR[:, k, c * P:(c + 1) * P], XTB[b][:, k, :], start=(k == 0), stop=(k == KC - 1))
                    last.then_inc(a["ps"], 1)
                for v in V_AFTER[b]:
                    values(v)

        def after(first, *waits):
            if not first:
                for eng, which, value in waits:
                    settle(eng, which, value)

        def settle(eng, which, value):
            if not isinstance(value, int):
                value = eng.to_reg(value)
                eng.wait_ge(which, 1)
            eng.wait_ge(which, value)

        def early(b, k, n):
            return isinstance(b, int) and b * NG + k < n

        ST_AT = {0: 0, 2: 1, 4: 2, 6: 3, 8: 4}
        PV_AT = {1: 2, 7: 0, 9: 1}
        OT_AT = 3
        MAXT_AT = 3
        AT_AT = {(2, 5): 0, (2, 9): 1}
        OUT_AT = {(2, 7): 0, (3, 1): 1}
        POST_AT = {(2, 8): 0, (3, 2): 1}
        NORM_AT = {(3, 0): 0, (3, 4): 1}
        XT_AT = {(3, 6): 0, (3, 8): 1}
        LOGITS_AT, GATE_AT, RANKS_AT = (0, 1), (0, 6), (0, 9)
        ROUTE_AT = {(0, 2): 0, (0, 3): 1, (0, 4): 2, (0, 5): 3, (0, 6): 4, (0, 7): 5, (1, 0): 6, (1, 1): 7, (1, 2): 8, (1, 3): 9, (1, 4): 10}

        SQUARES_AT = {1: 0, 9: 1}
        X1_HIGH_AT, X1_LOW_AT = (3, 6), (3, 8)
        SPLIT_AT = {(0, 7): 0, (0, 9): 1, (1, 1): 2, (1, 3): 3, (1, 5): 4, (1, 7): 5, (1, 9): 6}
        ACT_SPLITS = (7, 11), (11, 17), (17, 19), (19, NUNIT)
        DVE_SPLITS = (7, 15), (15, 16), (16, 17), (17, 19), (19, NUNIT)

        def last_steps(b):
            return isinstance(b, int) and b == B

        def live(b, k, lag):
            if not isinstance(b, int):
                return True
            return 0 <= b * NG + k - lag < NU

        LAST_AT, LAST_OUT, LAST_XT = bank[0:2], bank[2:4], bank[4:6]

        def granule(n):
            if n < 4:
                return ((n, 3, 0),)
            if n < 8:
                return (n - 4, 2, 0), (n - 4, 0, 3 * P)
            return (2 * (n - 8), 1, 0), (2 * (n - 8) + 1, 1, 2 * P)

        def slot_of(k, n):
            return (k * NTG + n) % 2

        @block.sync
        def _(sp):
            def load_unit(b, g):
                u = b * NG + g
                after(early(b, g, NG), (sp, s["ST"], (u - NG) * NTG + NTG))
                for which, dst, parts in ((1, K[g], KPART), (0, Q[g], QPART)):
                    for r, part in enumerate(parts):
                        src = qk_dram[which, part, g * GH * HD:(g + 1) * GH * HD, bass.ds(b * T, T)]
                        sp.dma_start(dst[r * HD:(r + 1) * HD, :, :], src.rearrange("(h d) t -> d h t", d=HD)).then_inc(s_kq[g], 16)

            def load_w1(n):
                at = n * 4 * UNIT
                sp.dma_start(W1[:, SPARE + at:SPARE + at + 4 * UNIT], w1T[:, at:at + 4 * UNIT]).then_inc(s_w1, 16)

            for b in range(B):
                for c in range(4):
                    sp.wait_ge(a["l"], 4 * b + c + 1)
                    sp.dma_start(qk_dram[c // 2, :, (c % 2) * P:(c % 2 + 1) * P, b * T:(b + 1) * T].rearrange("r p t -> p r t"),
                                 PB[c]).then_inc(s_pb[c], 16)
                if b == 0:
                    for c in range(4):
                        sp.wait_ge(s_pb[c], 16)
                load_unit(0, b)
            for c in range(4):
                sp.wait_ge(s_pb[c], 16 * B)
            sp.dma_start(XB[:, :, :], x[0:T, :].rearrange("(n p) f -> p n f", p=P)).then_inc(s_xb, 16)
            sp.wait_ge(a["v"], 8)
            for n in range(4):
                load_w1(n)
            for g in range(NG):
                load_unit(1, g)
                if g == 0:
                    sp.wait_ge(s_w1, 4 * 16)
                load_w1(4 + g)
            with sp.Fori(2, B) as b:
                for g in range(NG):
                    load_unit(b, g)
                    if g % 2 == 0:
                        at = ((b - 2) * 2 + g // 2) * (NX * E)
                        sp.dma_start(W2[:, bass.ds(at, NX * E)], w2T[:, bass.ds(at, NX * E)]).then_inc(s_w, 16)

        @block.gpsimd
        def _(pool):
            t = Tally()

            def link(ins):
                ins.then_inc(s["pool"], 1)
                settle(pool, s["pool"], t.step())

            def fill_v(b, k):
                v, g = b * NG + k - 1, (k - 1) % NG
                row = b if k else b - 1
                after(early(b, k, 3), (pool, s["pv"], (v - 2) * 3 + 3))
                for j in range(TT):
                    last = pool.tensor_copy(VA[g % 2][:, j, :, 0:HD],
                                            VR[:, bass.ds(row * TT + j, 1), g * GH * HD:(g + 1) * GH * HD].rearrange("p o (h d) -> p (o h) d", d=HD))
                last.then_inc(s["va"], 1)

            def maxima(b, g):
                u, p = b * NG + g, g % 2
                settle(pool, s["Sf"], (u + 1) * NSG)
                m = MX[p][:, :, :].rearrange("p h i -> p i h")
                part = [NP[p][:, :, r * GH:(r + 1) * GH] for r in range(PARTS)]
                link(pool.tensor_scalar(NM[:, 0, :, :], m, -1.0, None, ALU.mult))
                link(pool.tensor_copy(part[0], NM[:, 0, :, :]))
                link(pool.tensor_tensor(NM[:, 1, :, :], NM[:, 0, :, :], part[0], ALU.subtract))
                link(pool.tensor_copy(part[1], NM[:, 1, :, :]))
                pool.tensor_tensor(part[2], NM[:, 1, :, :], part[1], ALU.subtract).then_inc(s["np"], 1)
                settle(pool, s["np"], u + 1)

            def inverse_std(b, h):
                two = slice(2 * h, 2 * h + 2)
                settle(pool, s["var"], b * 2 + h + 1)
                link(pool.tensor_scalar(VE[:, two, :], MV[:, two, 1:2], EPS, None, ALU.add))
                pool.tensor_tensor(RS[:, two, :], VE[:, two, :], MHALF[:, :].unsqueeze(1).broadcast_to([P, 2, 1]), ALU.pow).then_inc(s["rs"], 1)

            def residual(b):
                after(early(b, 0, 1), (pool, s_x1w, b * 32))
                settle(pool, s_xb, b * 16 + 16)
                pool.tensor_tensor(XB[:, :, :], XB[:, :, :], BP[:, :].unsqueeze(1).broadcast_to([P, TT, E]), ALU.add).then_inc(s["xb"], 1)

            def scatter(r, part):
                if part == 0:
                    settle(pool, s_sc, r * (16 * TT * TOPK) + 16)
                    link(pool.tensor_copy(PAIR[:, :, :, 0], TOK[:, bass.ds(r * TT, TT)].unsqueeze(2).broadcast_to([P, TT, TOPK])))
                    settle(pool, s["slots"], r + 1)
                    settle(pool, s["wts"], r + 1)
                for n in range(2 * part, 2 * part + 2):
                    for k in range(TOPK):
                        pool.indirect_dma_start(tok_dram, bass.IndirectOffsetOnAxis(ap=SLI[:, n, k:k + 1], axis=0),
                                                PAIR[:, n, k, :], None).then_inc(s_sc, 16)

            pool.wait_ge(s_const, 10 * 16)
            pool.wait_ge(a["v"], 8)
            def step(b, k, tails=True, routing=True):
                if live(b, k, 1):
                    fill_v(b, k)
                if tails and k >= 2:
                    inverse_std(b - 1, k - 2)
                if routing and k == 1:
                    scatter(b - 2, 0)
                if live(b, k, 0):
                    maxima(b, k)
                if routing and k == 1:
                    scatter(b - 2, 1)
                if not early(b, k, NG) and k == 1:
                    residual(b - 1)

            for k in range(NG):
                step(0, k, False, False)
            for k in range(NG):
                step(1, k, routing=False)
            with pool.Fori(2, B) as b:
                t.enter(b - 2, 4 * NG + 2 + 1)
                for k in range(NG):
                    step(b, k)
                t.leave(B - 2)
            pool.wait_ge(s["f2"], 1)
            pool.tensor_tensor(ROOT[0][:, :], F2[1][:, :], MHALF[:, :], ALU.pow)
            pool.tensor_tensor(ROOT[1][:, :], F2[1][:, :], HALF[:, :], ALU.pow).then_inc(s["root"], 1)
            pool.wait_ge(s["root"], 1)
            pool.tensor_scalar(SW[:, :], ROOT[0][:, :], WSCALE, None, ALU.mult).then_inc(s["sc"], 1)
            pool.tensor_scalar(CW[:, :], ROOT[1][:, :], 1.0 / (WSCALE * XSCALE), None, ALU.mult).then_inc(s["sc"], 1)
            for k in range(2):
                step(B, k, tails=False)
            for h in range(2):
                inverse_std(B - 1, h)
            for part in range(2):
                scatter(B - 1, part)

        @block.scalar
        def _(act):
            def exps(b, k, n):
                v = b * NG + k - 2
                act.wait_ge(s["ST"], v * NTG + n + 1)
                after(early(b, k, 3), (act, s["pv"], (v - 1) * 3 + (1, 1, 2, 2, 3)[n]))
                act.activation(PT[n][:, :], STb[slot_of(k, n)].rearrange("p a n -> p (a n)"), ACT.Exp).then_inc(s["exp"], 1)

            def outputs(b, k):
                act.wait_ge(s["pv"], (b * NG + k - 3) * 3 + 3)
                act.activation(O[:, :], Ob, ACT.Copy).then_inc(s["ocp"], 1)

            def ao_columns(b, h, src):
                act.wait_ge(s["at"], b * 2 + h + 1)
                act.activation(XT1[:, 2 * h:2 * h + 2, :, :].rearrange("p n k t -> p (n k t)"), src, ACT.Copy).then_inc(s["atc"], 1)

            def x1_columns(b, h, src):
                act.wait_ge(s["tp"], b * 2 + h + 1)
                act.activation(XT1[:, 2 * h:2 * h + 2, :, :].rearrange("p n k t -> p (n k t)"), src, ACT.Copy).then_inc(s["xt"], 1)

            def gate_exp(b):
                act.wait_ge(s["dl"], b + 1)
                act.activation(EX[:, :], DL[:, :], ACT.Exp).then_inc(s["ex"], 1)

            def max_rows(b, k):
                u, g = b * NG + k, (k - 1) % NG
                act.wait_ge(s["mt"], u)
                act.activation(Q[g][SK:SKM, :, :], maxb[SK:SKM, 0:T].unsqueeze(1).broadcast_to([PARTS * GH, GH, T]),
                               ACT.Copy).then_inc(s["qm"], 1)

            def squares(b, i):
                c = (b - 2) * NX + i
                if i == 0:
                    settle(act, s_w1, (b - 1) * 64)
                settle(act, s["sq"], c + 1)
                act.activation(W1[:, 0:SPARE], W1[:, bass.ds(SPARE + c * 2 * UNIT, 2 * UNIT)], ACT.Square,
                               accum_out=SQ[:, bass.ds(c, 1)]).then_inc(s["sq"], 1)

            def weights_high(units):
                for u in range(*units):
                    if u == 0:
                        act.wait_ge(s["sc"], 2)
                    if u >= 2:
                        act.wait_ge(s["lo"], u - 1)
                    act.activation(w1h[:, 2 * u * UNIT:(2 * u + 1) * UNIT], W1[:, SPARE + u * UNIT:SPARE + (u + 1) * UNIT], ACT.Copy,
                                   scale=SW[:, :]).then_inc(s["hi"], 1)

            def x1_high(b):
                act.wait_ge(s["x1"], b * 2 + 2)
                act.activation(X1S[:, :, 0, :], X1[:, :, :], ACT.Copy, scale=XSCALE).then_inc(s["xh"], 1)

            def store_x1(b):
                act.wait_ge(s["xl"], b + 1)
                act.dma_start(x1_dram[bass.ds(b * T, T), :].rearrange("(n p) f -> p n f", p=P), X1S[:, :, :, :].rearrange("p n r f -> p n (r f)")).then_inc(s_x1w, 16)
                act.dma_start(acc_dram[bass.ds(b * T, T), :].rearrange("(n p) f -> p n f", p=P), X1[:, :, :]).then_inc(s_x1w, 16)

            def step(b, k, tails=True, routing=True):
                for n in range(NSG):
                    if n in ST_AT and live(b, k, 2):
                        exps(b, k, ST_AT[n])
                    if n == 1 and live(b, k, 3):
                        outputs(b, k)
                    if n == MAXT_AT and live(b, k, 1):
                        max_rows(b, k)
                    if routing and (k, n) == GATE_AT:
                        gate_exp(b - 2)
                    if tails and routing and n in SQUARES_AT:
                        squares(b, 2 * k + SQUARES_AT[n])
                    if last_steps(b) and (k, n) in SPLIT_AT:
                        weights_high((SPLIT_AT[k, n], SPLIT_AT[k, n] + 1))
                    if tails and (k, n) in AT_AT:
                        ao_columns(b - 1, AT_AT[k, n], MISC)
                    if tails and (k, n) in XT_AT:
                        x1_columns(b - 1, XT_AT[k, n], MISC)
                    if tails and (k, n) == X1_HIGH_AT:
                        x1_high(b - 1)
                if tails and k == 3:
                    store_x1(b - 1)
                    act.dma_start(XB[:, :, :], x[bass.ds(b * T, T), :].rearrange("(n p) f -> p n f", p=P)).then_inc(s_xb, 16)

            act.wait_ge(s_const, 10 * 16)
            for k in range(NG):
                step(0, k, False, False)
            for k in range(NG):
                step(1, k, routing=False)
            with act.Fori(2, B) as b:
                for k in range(NG):
                    step(b, k)
            for k in range(3):
                step(B, k, tails=False)
            weights_high(ACT_SPLITS[0])
            for h in range(2):
                ao_columns(B - 1, h, LAST_AT[h])
            weights_high(ACT_SPLITS[1])
            for h in range(2):
                x1_columns(B - 1, h, LAST_XT[h])
            x1_high(B - 1)
            weights_high(ACT_SPLITS[2])
            store_x1(B - 1)
            gate_exp(B - 1)
            weights_high(ACT_SPLITS[3])
            act.wait_ge(s["ex"], B)
            act.activation(EX0[:, :], ONE[:, :], ACT.Silu)

        @block.vector
        def _(dve):
            t = Tally()

            def link(ins):
                ins.then_inc(s["dve"], 1)
                settle(dve, s["dve"], t.step())

            def reduces(b, k, n):
                u, p = b * NG + k, k % 2
                settle(dve, s["S"], u * NSG + n + 1)
                if n == 0:
                    after(early(b, k, 2), (dve, s["np"], u - 1))
                for h, i, at in granule(n):
                    w = (i + 1) * P
                    src = Sb[n % 2][:, at:at + w]
                    last = dve.tensor_tensor_reduce(src, src, maskS[:, TT * P - w:], 1.0, LOW, ALU.add, ALU.max, MX[p][:, h, i:i + 1])
                last.then_inc(s["Sf"], 1)

            def normalise(b, k):
                w, g = b * NG + k - 3, (k - 3) % NG
                dve.wait_ge(s["ot"], w + 1)
                dve.reciprocal(RC[:, :, :, :], Ot[:, :, :, HD:HD + 1]).then_inc(s["rc"], 1)
                dve.wait_ge(s["rc"], w + 1)
                if k == 3 and not early(b, k, NG):
                    dve.wait_ge(s["at"], b * 2)
                dve.tensor_tensor(AO[:, :, g * GH * HD:(g + 1) * GH * HD].rearrange("p i (h d) -> p i h d", d=HD), Ot[:, :, :, 0:HD],
                                  RC[:, :, :, :].broadcast_to([P, TT, GH, HD]), ALU.mult).then_inc(s["nrm"], 1)

            def post(b, h, src):
                dve.wait_ge(s["ap"], b * 2 + h + 1)
                if h == 0:
                    dve.wait_ge(s["xb"], b + 1)
                two = slice(2 * h, 2 * h + 2)
                dve.tensor_tensor(XB[:, two, :], src.rearrange("p (n f) -> p n f", n=2), XB[:, two, :], ALU.add).then_inc(s["res"], 1)
                dve.wait_ge(s["res"], b * 2 + h + 1)
                for n in (2 * h, 2 * h + 1):
                    last = dve.bn_stats(ST6[:, n, :], XB[:, n, :])
                link(last)
                for n in (2 * h, 2 * h + 1):
                    last = dve.bn_aggr(MV[:, n, :], ST6[:, n, :])
                last.then_inc(s["var"], 1)

            def normal_rows(b, h):
                dve.wait_ge(s["rs"], b * 2 + h + 1)
                for n in (2 * h, 2 * h + 1):
                    last = dve.tensor_scalar(X1[:, n, :], XB[:, n, :], MV[:, n, 0:1], RS[:, n, :], ALU.subtract, ALU.mult)
                last.then_inc(s["x1"], 1)

            def mark(ins):
                ins.then_inc(s["dve"], 1)
                return t.step()

            done = {}

            def route(r, part):
                if part == 0:
                    dve.wait_ge(s["lgp"], r + 1)
                    dve.tensor_copy(LG[:, :, :], MISC[:, 0:TT * NX].rearrange("p (n e) -> p n e", e=NX)).then_inc(s["lg"], 1)
                elif part == 1:
                    settle(dve, s["lg"], r + 1)
                    for n in range(TT):
                        last = dve.max(MVX[:, n, :], LG[:, n, :])
                    done["max"] = mark(last)
                elif part == 2:
                    settle(dve, s["dve"], done["max"])
                    for n in range(TT):
                        last = dve.max_index(MIX[:, n, :], MVX[:, n, :], LG[:, n, :])
                    done["index"] = mark(last)
                elif part == 3:
                    settle(dve, s["dve"], done["index"])
                    dve.tensor_tensor(DL[:, :], MVX[:, :, 1], MVX[:, :, 0], ALU.subtract).then_inc(s["dl"], 1)
                    done["float"] = mark(dve.tensor_copy(MIF[:, :, :], MIX[:, :, :]))
                elif part == 4:
                    settle(dve, s["dve"], done["float"])
                    for k in range(TOPK):
                        last = dve.tensor_tensor(OH[k][:, :, :], iota8.unsqueeze(1).broadcast_to([P, TT, NX]),
                                                 MIF[:, :, k:k + 1].broadcast_to([P, TT, NX]), ALU.is_equal)
                    done["hot"] = mark(last)
                elif part == 5:
                    settle(dve, s["dve"], done["hot"])
                    dve.tensor_tensor(MC[:, :, :], OH[0][:, :, :], OH[1][:, :, :], ALU.add).then_inc(s["mc"], 1)
                elif part == 6:
                    dve.wait_ge(s["rkp"], r + 1)
                    dve.tensor_tensor(RK[:, :, :], MISC[:, 0:TT * NX].rearrange("p (n e) -> p n e", e=NX),
                                      ebase8.unsqueeze(1).broadcast_to([P, TT, NX]), ALU.add).then_inc(s["rk"], 1)
                elif part == 7:
                    dve.wait_ge(s["rk"], r + 1)
                    for k in range(TOPK):
                        last = dve.tensor_tensor(RKO[k][:, :, :], RK[:, :, :], OH[k][:, :, :], ALU.mult)
                    done["slot"] = mark(last)
                    dve.wait_ge(s["ex"], r + 1)
                    done["sum"] = mark(dve.tensor_scalar(SM[:, :], EX[:, :], 1.0, None, ALU.add))
                elif part == 8:
                    settle(dve, s_sc, r * (16 * TT * TOPK) + 16)
                    settle(dve, s["dve"], done["slot"])
                    for k in range(TOPK):
                        last = dve.tensor_reduce(SLF[:, :, k], RKO[k][:, :, :], AX.X, ALU.add)
                    done["slot"] = mark(last)
                    settle(dve, s["dve"], done["sum"])
                    done["first"] = mark(dve.reciprocal(PAIRF[:, :, 0, 1], SM[:, :]))
                elif part == 9:
                    settle(dve, s["dve"], done["slot"])
                    dve.tensor_copy(SLI[:, :, :], SLF[:, :, :]).then_inc(s["slots"], 1)
                    settle(dve, s["dve"], done["first"])
                    dve.tensor_tensor(PAIRF[:, :, 1, 1], PAIRF[:, :, 0, 1], EX[:, :], ALU.mult).then_inc(s["wts"], 1)
                    done["count"] = mark(dve.tensor_reduce(MSUM[:, :], MC[:, :, :].rearrange("p n e -> p e n"), AX.X, ALU.add))
                elif part == 10:
                    settle(dve, s["dve"], done["count"])
                    dve.tensor_tensor(MRUN[:, :], MRUN[:, :], MSUM[:, :], ALU.add).then_inc(s["mrun"], 1)

            def weights_low(units):
                for u in range(*units):
                    dve.wait_ge(s["hi"], u + 1)
                    dve.scalar_tensor_tensor(w1h[:, (2 * u + 1) * UNIT:(2 * u + 2) * UNIT], W1[:, SPARE + u * UNIT:SPARE + (u + 1) * UNIT], SW[:, :],
                                             w1h[:, 2 * u * UNIT:(2 * u + 1) * UNIT], ALU.mult, ALU.subtract).then_inc(s["lo"], 1)

            def x1_low(b):
                settle(dve, s["xh"], b + 1)
                dve.scalar_tensor_tensor(X1S[:, :, 1, :], X1[:, :, :], XSCALE, X1S[:, :, 0, :], ALU.mult, ALU.subtract).then_inc(s["xl"], 1)

            def step(b, k, tails=True, routing=True):
                for n in range(NSG):
                    if live(b, k, 0):
                        reduces(b, k, n)
                    if n == OT_AT + 1 and live(b, k, 3):
                        normalise(b, k)
                    if tails and (k, n) in POST_AT:
                        post(b - 1, POST_AT[k, n], MISC)
                    if tails and (k, n) in NORM_AT:
                        normal_rows(b - 1, NORM_AT[k, n])
                    if routing and (k, n) in ROUTE_AT:
                        route(b - 2, ROUTE_AT[k, n])
                    if tails and (k, n) == X1_LOW_AT:
                        x1_low(b - 1)
                    if last_steps(b) and (k, n) in SPLIT_AT:
                        weights_low((SPLIT_AT[k, n], SPLIT_AT[k, n] + 1))

            dve.wait_ge(s_const, 10 * 16)
            dve.tensor_copy(IDH[:, :], ident)
            dve.wait_ge(s_zero, 2 * 16)
            for k in range(NG):
                step(0, k, False, False)
            for k in range(NG):
                step(1, k, routing=False)
            with dve.Fori(2, B) as b:
                t.enter(b - 2, 2 + 4 + 5)
                for k in range(NG):
                    step(b, k)
                t.leave(B - 2)
            dve.wait_ge(s["sqp"], 1)
            link(dve.tensor_reduce(F2[0][:, :], bank[0][:, 0:KC * NX], AX.X, ALU.add))
            dve.tensor_scalar(F2[1][:, :], F2[0][:, :], 1e-30, None, ALU.max).then_inc(s["f2"], 1)
            for k in range(3):
                step(B, k, tails=False)
            weights_low(DVE_SPLITS[0])
            for h in range(2):
                post(B - 1, h, LAST_OUT[h])
            weights_low(DVE_SPLITS[1])
            for h in range(2):
                normal_rows(B - 1, h)
            weights_low(DVE_SPLITS[2])
            x1_low(B - 1)
            weights_low(DVE_SPLITS[3])
            for part in range(11):
                route(B - 1, part)
            dve.wait_ge(s["cnt"], 1)
            link(dve.tensor_copy(NF[:, :], MISC[:, 0:NX]))
            link(dve.tensor_tensor(GE[:, :, :], NF[:, :].unsqueeze(2).broadcast_to([P, NX, 16]),
                                   thr16.unsqueeze(1).broadcast_to([P, NX, 16]), ALU.is_gt))
            link(dve.tensor_reduce(NT[:, :], GE[:, :, :], AX.X, ALU.add))
            link(dve.tensor_tensor(G8[:, :, :], tri8.rearrange("p (a b) -> p a b", a=NX),
                                   NT[:, :].unsqueeze(1).broadcast_to([P, NX, NX]), ALU.mult))
            link(dve.tensor_reduce(CT[:, :], G8[:, :, :], AX.X, ALU.add))
            link(dve.tensor_tensor(GJ[:, :, :], CT[0:1, :].unsqueeze(1).broadcast_to([1, NTAB, NX]),
                                   jidx[0:1, :].unsqueeze(2).broadcast_to([1, NTAB, NX]), ALU.is_le))
            link(dve.tensor_reduce(EJ[:, :], GJ[:, :, :], AX.X, ALU.add))
            link(dve.tensor_tensor(GP[:, :, :], GJ[:, :, :], NT[0:1, :].unsqueeze(1).broadcast_to([1, NTAB, NX]), ALU.mult))
            link(dve.tensor_reduce(PJ[:, :], GP[:, :, :], AX.X, ALU.add))
            link(dve.tensor_tensor(PJ[:, :], jidx[0:1, :], PJ[:, :], ALU.subtract))
            link(dve.tensor_scalar(PJ[:, :], PJ[:, :], float(P), None, ALU.mult))
            link(dve.scalar_tensor_tensor(RJ[:, :], EJ[:, :], float(REGION), PJ[:, :], ALU.mult, ALU.add))
            link(dve.tensor_copy(TAB[:, 0, :], RJ[:, :]))
            dve.tensor_scalar(TAB[:, 1, :], EJ[:, :], float(NX - 1), None, ALU.min).then_inc(s["tab"], 1)
            weights_low(DVE_SPLITS[4])

        @block.tensor
        def _(pe):
            mm = nc.tensor.matmul

            def S(b, k, n):
                u, p = b * NG + k, k
                if n == 0:
                    pe.wait_ge(s_kq[k], (b + 1) * (16 * 2 * len(QPART)))
                after(early(b, k, 1) and n < 2, (pe, s["Sf"], u * NSG + n - 1))
                dst = Sb[n % 2]

                for h, i, at in granule(n):
                    w = (i + 1) * P
                    last = mm(dst[:, at:at + w], Q[p][0:SK, h, i * P:(i + 1) * P], K[p][0:SK, h, 0:w], start=True, stop=True)
                last.then_inc(s["S"], 1)

            def where(h, j):
                if j == 2:
                    return 4, h // 2, 2 * P * (h % 2)
                return (0 if j == 0 else 2) + h // 2, h % 2, (0, 0, 0, 3 * P)[j]

            def ST(b, k, n):
                v, g = b * NG + k - 2, (k - 2) % NG
                if n == 0:
                    pe.wait_ge(s["qm"], v + 1)
                after(early(b, k, 3) and n < 2, (pe, s["exp"], v * NTG + n - 1))
                for h in range(GH):
                    for j in range(TT):
                        gr, bk, at = where(h, j)
                        if gr != n:
                            continue
                        dst = STb[slot_of(k, n)][:, bk, :]
                        mm(dst[:, at:at + T - j * P], K[g][0:SKM, h, j * P:(j + 1) * P], Q[g][0:SKM, h, j * P:T], start=True, stop=False)
                        last = mm(dst[:, at:at + P], identb, maskT, start=False, stop=True)
                last.then_inc(s["ST"], 1)

            def PV(b, k, n, lag=2):
                v, p = b * NG + k - lag, (k - lag) % 2
                pe.wait_ge(s["exp"], v * NTG + (2, 4, 5)[n])
                if n == 0:
                    pe.wait_ge(s["va"], v + 1)
                    if live(b, k, 1):
                        pe.wait_ge(s["qm"], v + 2)
                    else:
                        pe.wait_ge(s["ocp"], v)
                for j in ((0,), (1, 3), (2,))[n]:
                    for h in range(GH):
                        gr, bk, at = where(h, j)
                        last = mm(Ob[32 * h:32 * h + 32, j * P:T], VA[p][:, j, h, :], PT[gr][:, bk * T + at:bk * T + at + T - j * P],
                                  start=(j == 0), stop=(j == 2), tile_position=(0, 32 * h))
                last.then_inc(s["pv"], 1)

            def maxT(b, k):
                u, p = b * NG + k, (k - 1) % 2
                after(early(b, k, 3), (pe, s["ocp"], u - 2))
                pe.wait_ge(s["np"], u)
                for i in range(TT):
                    last = nc.tensor.transpose(maxb[SK:SKM, i * P:(i + 1) * P], NP[p][:, i, :], identb, tile_position=(0, SK))
                last.then_inc(s["mt"], 1)

            def outputs_T(b, k, last_reader):
                if last_reader:
                    pe.wait_ge(*last_reader)
                pe.wait_ge(s["ocp"], b * NG + k - 2)
                for i in range(TT):
                    last = nc.tensor.transpose(MISC[:, i * P:(i + 1) * P], O[:, i * P:(i + 1) * P], ident)
                last.then_inc(s["ot"], 1)

            def ao_T(b, h, last_reader, dst=MISC):
                if last_reader:
                    pe.wait_ge(*last_reader)
                for n in range(2):
                    for k in range(KC):
                        last = nc.tensor.transpose(dst[:, (n * KC + k) * P:(n * KC + k + 1) * P], AO[:, 2 * h + n, k * P:(k + 1) * P], ident)
                last.then_inc(s["at"], 1)

            def out_proj(b, h, last_reader, dst=MISC):
                pe.wait_ge(*last_reader)
                for n in range(2):
                    for k in range(KC):
                        last = mm(dst[:, n * E:(n + 1) * E], XT1[:, 2 * h + n, k, :], WP[:, k, :], start=(k == 0), stop=(k == KC - 1))
                last.then_inc(s["ap"], 1)

            def x1_T(b, h, last_reader, dst=MISC):
                if last_reader:
                    pe.wait_ge(*last_reader)
                pe.wait_ge(s["x1"], b * 2 + h + 1)
                for n in range(2):
                    for k in range(KC):
                        last = nc.tensor.transpose(dst[:, (n * KC + k) * P:(n * KC + k + 1) * P], X1[:, 2 * h + n, k * P:(k + 1) * P], ident)
                last.then_inc(s["tp"], 1)

            def logits(b, last_reader):
                if last_reader:
                    pe.wait_ge(*last_reader)
                for n in range(TT):
                    if n % 2 == 0 and not last_reader:
                        pe.wait_ge(s["xt"], b * 2 + n // 2 + 1)
                    for k in range(KC):
                        last = mm(MISC[:, n * NX:(n + 1) * NX], XT1[:, n, k, :], RW[:, k, :], start=(k == 0), stop=(k == KC - 1))
                last.then_inc(s["lgp"], 1)

            def ranks(b, last_reader):
                pe.wait_ge(*last_reader)
                pe.wait_ge(s["mc"], b + 1)
                pe.wait_ge(s["mrun"], b + 1)
                for n in range(TT):
                    dst = MISC[:, n * NX:(n + 1) * NX]
                    mm(dst, tri, MC[:, n, :], start=True, stop=False)
                    for m in range(n):
                        mm(dst, onesb, MC[:, m, :], start=False, stop=False)
                    last = mm(dst, onesb, MRUN[:, :], start=False, stop=True)
                last.then_inc(s["rkp"], 1)

            def step(b, k, tails=True, routing=True):
                u, r = b * NG + k, b - 1
                if k == 3 and tails:
                    reader = (s["atc"], r * 2 + 2)
                elif k == 0 and routing:
                    reader = (s["xt"], r * 2)
                elif k == 1 and routing:
                    reader = (s["rk"], r)
                else:
                    reader = None if early(b, k, 4) else (s["nrm"], u - 3)
                for n in range(NSG):
                    if live(b, k, 0):
                        S(b, k, n)
                    if n in ST_AT and live(b, k, 2):
                        ST(b, k, ST_AT[n])
                    if n in PV_AT and live(b, k, 3 if n == 1 else 2):
                        PV(b, k, PV_AT[n], 3 if n == 1 else 2)
                    if routing and (k, n) == LOGITS_AT:
                        logits(b - 2, reader)
                        reader = (s["lg"], r)
                    if n == OT_AT and live(b, k, 3):
                        outputs_T(b, k, reader)
                        reader = (s["nrm"], u - 2)
                    if n == MAXT_AT and live(b, k, 1):
                        maxT(b, k)
                    if tails and (k, n) in AT_AT:
                        h = AT_AT[k, n]
                        ao_T(r, h, reader)
                        reader = (s["atc"], r * 2 + h + 1)
                    if tails and (k, n) in OUT_AT:
                        h = OUT_AT[k, n]
                        out_proj(r, h, reader)
                        reader = (s["res"], r * 2 + h + 1)
                    if tails and (k, n) in XT_AT:
                        h = XT_AT[k, n]
                        x1_T(r, h, reader)
                        reader = (s["xt"], r * 2 + h + 1)
                    if routing and (k, n) == RANKS_AT:
                        ranks(b - 2, reader)

            pe.wait_ge(s_const, 10 * 16)
            pe.wait_ge(a["qf"], 4 * B)
            pe.wait_ge(a["v"], 8)
            for k in range(NG):
                step(0, k, False, False)
            for k in range(NG):
                step(1, k, routing=False)
            with pe.Fori(2, B) as b:
                for k in range(NG):
                    step(b, k)
            pe.wait_ge(s["sq"], KC * NX + 1)
            pe.wait_ge(s["Sf"], NU * NSG)
            mm(bank[0][:, 0:KC * NX], ONESF[:, :], SQ[:, :], start=True, stop=True).then_inc(s["sqp"], 1)
            for k in range(3):
                step(B, k, tails=False)
            r = B - 1
            for h in range(2):
                ao_T(r, h, (s["nrm"], NU), LAST_AT[h])
            for h in range(2):
                out_proj(r, h, (s["atc"], r * 2 + h + 1), LAST_OUT[h])
            for h in range(2):
                x1_T(r, h, None, LAST_XT[h])
            logits(r, None)
            ranks(r, (s["lg"], B))
            pe.wait_ge(s["rk"], B)
            pe.wait_ge(s["mrun"], B + 1)
            mm(MISC[:, 0:NX], onesb, MRUN[:, :], start=True, stop=True).then_inc(s["cnt"], 1)

        f = {n: sem("c_" + n) for n in ("xt", "xgt", "g", "u", "sil", "h", "th", "ht", "yp", "ys", "idw")}
        s_idx, s_g = ([sem(f"s_{n}{q}") for q in range(TRIO)] for n in ("idx", "xg"))
        s_acc = sem("s_acc")
        NTRIO = NTILES // TRIO
        G, U, XP, HP, YP = bank[0], bank[1], bank[2], bank[3], bank[4]
        XPh = XP.bitcast(F16)

        @block.sync
        def _(sp):
            def first_slot(j):
                return sp.value_load(TAB[0:1, 0, bass.ds(j, 1)], min_val=0, max_val=NSLOT - P)

            def fetch_tokens(i, q):
                at = first_slot(i * TRIO + q)
                sp.dma_start(IDX[q][:, :], tok_dram[bass.ds(at, P), :]).then_inc(s_idx[q], 16)

            sp.wait_ge(s["tab"], 1)
            sp.wait_ge(s_sc, 16 * TT * TOPK * B + 16)
            for q in range(TRIO):
                fetch_tokens(0, q)
            with sp.Fori(0, NTRIO) as i:
                for q in range(TRIO):
                    sp.wait_ge(f["idw"], i * TRIO + q + 1)
                    fetch_tokens(i + 1, q)
            for q in range(TRIO):
                sp.wait_ge(s_idx[q], 16 * (NTRIO + 1))

        @block.gpsimd
        def _(pool):
            def gather(i, q):
                settle(pool, s_idx[q], i * 16 + 16)
                pool.indirect_dma_start(XG[q], None, x1_dram, bass.IndirectOffsetOnAxis(ap=IDX[q][:, 0:1], axis=0)).then_inc(s_g[q], 16)

            def keep_index(i, q):
                settle(pool, s_g[q], i * 16 + 16)
                pool.tensor_copy(IDW[q][:, :], IDX[q][:, :]).then_inc(f["idw"], 1)

            def add_result(j, q):
                settle(pool, f["ys"], j + 1)
                after(isinstance(j, int) and j == 0, (pool, s_acc, j * 16))
                pool.indirect_dma_start(acc_dram, bass.IndirectOffsetOnAxis(ap=IDW[q][:, 0:1], axis=0), YS[q], None,
                                        compute_op=ALU.add).then_inc(s_acc, 16)

            def trio(i):
                for q in range(TRIO):
                    j = i * TRIO + q
                    settle(pool, f["xt"], j + 1)
                    gather(i + 1, q)
                    if q or not isinstance(i, int):
                        add_result(j - 1, (q - 1) % TRIO)
                    if q < TRIO - 1:
                        keep_index(i, q + 1)
                    else:
                        keep_index(i + 1, 0)

            pool.wait_ge(s_x1w, 32 * B)
            pool.wait_ge(s_zero, 2 * 16)
            pool.wait_ge(s["pv"], 3 * NU)
            for q in range(TRIO):
                gather(0, q)
            keep_index(0, 0)
            trio(0)
            with pool.Fori(1, NTRIO) as i:
                trio(i)
            add_result(NTILES - 1, TRIO - 1)

        @block.scalar
        def _(act):
            def columns(j, q):
                act.wait_ge(f["xt"], j + 1)
                act.activation(XGT[q].rearrange("p r k t -> p (r k t)"), XPh[:, 0:2 * E], ACT.Copy).then_inc(f["xgt"], 1)

            def silu(j):
                act.wait_ge(f["g"], j + 1)
                act.activation(SIL, G, ACT.Silu, scale=CW[:, :]).then_inc(f["sil"], 1)

            def result(i, q, j):
                act.wait_ge(f["yp"], j + 1)
                act.wait_ge(f["idw"], j + 1)
                after(isinstance(i, int) and i == 0, (act, s_acc, (j - TRIO + 1) * 16))
                act.activation(YS[q], YP[:, 0:E], ACT.Copy, scale=IDW[q][:, 1:2].bitcast(F32)).then_inc(f["ys"], 1)

            def tile_(i, q):
                j = i * TRIO + q
                columns(j + 1, (q + 1) % TRIO)
                silu(j)
                if q:
                    result(i, q - 1, j - 1)
                elif not (isinstance(i, int) and i == 0):
                    result(i - 1, TRIO - 1, j - 1)

            columns(0, 0)
            for i in range(2):
                for q in range(TRIO):
                    tile_(i, q)
            with act.Fori(2, NTRIO) as i:
                for q in range(TRIO):
                    tile_(i, q)
            result(NTRIO - 1, TRIO - 1, NTILES - 1)

        @block.vector
        def _(dve):
            def tile_(j):
                dve.wait_ge(f["sil"], j + 1)
                dve.wait_ge(f["u"], j + 1)
                after(isinstance(j, int) and j == 0, (dve, f["th"], j))
                dve.scalar_tensor_tensor(HH, U, CW[:, :], SIL, ALU.mult, ALU.mult).then_inc(f["h"], 1)
                dve.wait_ge(f["th"], j + 1)
                after(isinstance(j, int) and j == 0, (dve, f["yp"], j))
                dve.tensor_copy(HT.rearrange("p k t -> p (k t)"), HP).then_inc(f["ht"], 1)

            tile_(0)
            with dve.Fori(1, NTILES) as j:
                tile_(j)

        @block.tensor
        def _(pe):
            mm = nc.tensor.matmul

            def expert(j):
                return pe.value_load(TAB[0:1, 1, bass.ds(j, 1)], min_val=0, max_val=NX - 1)

            def rows_T(i, q, j):
                pe.wait_ge(s_g[q], i * 16 + 16)
                after(isinstance(j, int) and j == 0, (pe, f["xgt"], j))
                for k in range(2 * KC):
                    last = nc.tensor.transpose(XPh[:, k * P:(k + 1) * P], XG[q][:, k * P:(k + 1) * P], IDH[:, :])
                last.then_inc(f["xt"], 1)

            def half(j, q, e, dst, n, done, used):
                after(isinstance(j, int) and j == 0, (pe, used, j))
                for k in range(KC):
                    for x_part, w_part in ((0, 0), (0, 1), (1, 0)):
                        at = (e + k * NX) * (4 * UNIT) + (2 * n + w_part) * UNIT
                        last = mm(dst, XGT[q][:, x_part, k, :], w1h[:, bass.ds(at, UNIT)], start=(k == x_part == w_part == 0), stop=(k == KC - 1 and x_part == 1))
                last.then_inc(done, 1)

            def gate(j, q, e):
                pe.wait_ge(f["xgt"], j + 1)
                half(j, q, e, G, 0, f["g"], f["sil"])

            def up(j, q, e):
                half(j, q, e, U, 1, f["u"], f["h"])

            def hidden_T(j):
                pe.wait_ge(f["h"], j + 1)
                after(isinstance(j, int) and j == 0, (pe, f["ht"], j))
                for k in range(FF // P):
                    last = nc.tensor.transpose(HP[:, k * P:(k + 1) * P], HH[:, k * P:(k + 1) * P], ident)
                last.then_inc(f["th"], 1)

            def down(j, e):
                pe.wait_ge(f["ht"], j + 1)
                after(isinstance(j, int) and j == 0, (pe, f["ys"], j))
                for k in range(FF // P):
                    last = mm(YP[:, 0:E], HT[:, k, :], W2[:, bass.ds((e + k * NX) * E, E)], start=(k == 0), stop=(k == FF // P - 1))
                last.then_inc(f["yp"], 1)

            def trio(i):
                e_before = None
                for q in range(TRIO):
                    j = i * TRIO + q
                    e = expert(j)
                    gate(j, q, e)
                    if q < TRIO - 1:
                        rows_T(i, q + 1, j + 1)
                    else:
                        rows_T(i + 1, 0, j + 1)
                    up(j, q, e)
                    if q:
                        down(j - 1, e_before)
                    elif not isinstance(i, int):
                        down(j - 1, expert(j - 1))
                    hidden_T(j)
                    e_before = e

            pe.wait_ge(s["tab"], 1)
            pe.wait_ge(s_w, 16 * (FF // P))
            pe.wait_ge(s["lo"], NUNIT)
            pe.wait_ge(s["exp"], NU * NTG)
            pe.wait_ge(s["Sf"], NU * NSG)
            rows_T(0, 0, 0)
            trio(0)
            with pe.Fori(1, NTRIO) as i:
                trio(i)
            down(NTILES - 1, expert(NTILES - 1))

        d = {n: sem("d_" + n) for n in ("stat", "var", "ve", "rs", "nm", "out")}
        CTILES = 2
        NCHUNK = NTT // CTILES
        s_in, s_out = [sem(f"s_in{c}") for c in range(NCHUNK)], sem("s_out")
        YB = [PT[c // 2][:, c % 2 * CTILES * E:(c % 2 + 1) * CTILES * E].rearrange("p (n f) -> p n f", n=CTILES) for c in range(NCHUNK)]
        ST = sb("ST", [P, NTT, 6])
        MVA = sb("MVA", [P, NTT, 2])
        VEA = sb("VEA", [P, NTT, 1])
        RSA = sb("RSA", [P, NTT, 1])
        NMA = sb("NMA", [P, NTT, 1])

        @block.sync
        def _(sp):
            sp.wait_ge(s_acc, 16 * NTILES)
            for q in range(TRIO):
                sp.wait_ge(s_g[q], 16 * (NTRIO + 1))
            for c in range(NCHUNK):
                sp.dma_start(YB[c], acc_dram[c * CTILES * P:(c + 1) * CTILES * P, :].rearrange("(n p) f -> p n f", p=P)).then_inc(s_in[c], 16)
            for c in range(NCHUNK):
                sp.wait_ge(d["out"], c + 1)
                sp.dma_start(out[c * CTILES * P:(c + 1) * CTILES * P, :].rearrange("(n p) f -> p n f", p=P), YB[c]).then_inc(s_out, 16)
            sp.wait_ge(s_out, 16 * NCHUNK)

        @block.gpsimd
        def _(pool):
            for c in range(NCHUNK):
                row = slice(c * CTILES, (c + 1) * CTILES)
                pool.wait_ge(d["ve"], c + 1)
                pool.tensor_tensor(RSA[:, row, :], VEA[:, row, :], MHALF[:, :].unsqueeze(1).broadcast_to([P, CTILES, 1]), ALU.pow).then_inc(d["rs"], 1)

        @block.vector
        def _(dve):
            def statistics(c):
                dve.wait_ge(s_in[c], 16)
                for n in range(CTILES):
                    last = dve.bn_stats(ST[:, c * CTILES + n, :], YB[c][:, n, :])
                last.then_inc(d["stat"], 1)
                dve.wait_ge(d["stat"], c + 1)
                for n in range(CTILES):
                    last = dve.bn_aggr(MVA[:, c * CTILES + n, :], ST[:, c * CTILES + n, :])
                last.then_inc(d["var"], 1)
                dve.wait_ge(d["var"], c + 1)
                row = slice(c * CTILES, (c + 1) * CTILES)
                dve.tensor_scalar(VEA[:, row, :], MVA[:, row, 1:2], EPS, None, ALU.add).then_inc(d["ve"], 1)

            def shift(c):
                row = slice(c * CTILES, (c + 1) * CTILES)
                dve.wait_ge(d["rs"], c + 1)
                dve.scalar_tensor_tensor(NMA[:, row, :], MVA[:, row, 0:1], -1.0, RSA[:, row, :], ALU.mult, ALU.mult).then_inc(d["nm"], 1)

            statistics(0)
            for c in range(1, NCHUNK):
                statistics(c)
                shift(c - 1)
            shift(NCHUNK - 1)

        @block.scalar
        def _(act):
            for c in range(NCHUNK):
                act.wait_ge(d["nm"], c + 1)
                for n in range(CTILES):
                    m = c * CTILES + n
                    last = act.activation(YB[c][:, n, :], YB[c][:, n, :], ACT.Identity, bias=NMA[:, m, :], scale=RSA[:, m, :])
                last.then_inc(d["out"], 1)


def constants():
    f32 = np.float32
    cf = np.zeros((P, 224 + NTAB), f32)
    cf[:, 0:P] = np.eye(P)
    cf[:, 128:136] = np.arange(NX)
    cf[:, 136:144] = np.arange(NX) * REGION
    cf[:, 144:160] = np.arange(16) * P
    cf[:, 160:224] = np.tril(np.ones((NX, NX))).reshape(-1)
    cf[:, 224:224 + NTAB] = np.arange(NTAB)
    bf = np.dtype("bfloat16")
    row, col = np.arange(P)[:, None], np.arange(P)[None, :]
    low = f32(-1e30)
    cb = np.concatenate([row == col, (row > col) * low, row < col, np.ones((P, P)), np.zeros((P, 3 * P)), (col > row) * low], 1).astype(bf)
    kones = np.zeros((PARTS * GH, GH, T), bf)
    for r in range(PARTS):
        for h in range(GH):
            kones[r * GH + h, h, :] = 1
    freqs = f32(10000.0) ** (-(np.arange(0, HD, 2, dtype=f32) / f32(HD)))
    angle = np.outer(np.arange(H, dtype=f32), freqs).astype(f32).reshape(1, -1)
    cos_sin = np.concatenate([np.cos(angle), np.sin(angle)], 0).astype(f32)
    tokid = (np.arange(NTT)[None, :] * P + np.arange(P)[:, None]).astype(np.int32)
    unused = np.zeros((NSLOT, 2), np.int32)
    unused[:, 0] = NTOK + np.arange(NSLOT) % P
    return cf, cb, kones, cos_sin, tokid, unused


def kernel(**inputs):
    import concourse.bacc as _bacc
    from concourse.bass_utils import run_bass_kernel_spmd as _run

    a = {k: np.asarray(v) for k, v in inputs.items()}
    x = a["L0_attn_x"].reshape(NTOK, E)
    cf, cb, kones, cos_sin, tokid, unused = constants()
    arrays = {
        "x": x, "xT": x.T, "w_attn": a["L0_attn_w_attn"], "b_attn": a["L0_attn_b_attn"], "w_proj": a["L0_attn_w_proj"].reshape(KC, P, E),
        "b_proj": a["L0_attn_b_proj"], "router_wT": a["L0_ffn_router_w"].T,
        "w1T": a["L0_ffn_ws"].transpose(2, 0, 1).reshape(KC, P, NX, 2 * FF).transpose(1, 0, 2, 3).reshape(P, -1),
        "w2T": a["L0_ffn_w2s"].transpose(2, 0, 1).reshape(FF // P, P, NX, E).transpose(1, 0, 2, 3).reshape(P, -1),
        "cos_sin": cos_sin, "cf": cf, "cb": cb, "kones": kones, "tokid": tokid, "unused": unused,
    }
    arrays = {k: np.ascontiguousarray(v) for k, v in arrays.items()}
    nc = _bacc.Bacc("TRN2", target_bir_lowering=False, num_devices=1)
    args = {k: nc.dram_tensor(k, v.shape, mybir.dt.from_np(v.dtype), kind="ExternalInput").ap() for k, v in arrays.items()}
    out = nc.dram_tensor("out", (NTOK, E), F32, kind="ExternalOutput").ap()
    block_kernel(nc, out=out, **args)
    r = _run(nc, [arrays], core_ids=[0])
    return r.results[0]["out"].reshape(B, T, E)
```
